# Optimizing a Trainium2 kernel written in Bass

```python
import numpy as np
import jax
import jax.numpy as jnp

def _softmax(x, axis=-1):
    return jax.nn.softmax(x, axis=axis)

def _gelu(x):
    return jax.nn.gelu(x, approximate=True)

def _silu(x):
    return jax.nn.silu(x)

def _sigmoid(x):
    return jax.nn.sigmoid(x)

def _layernorm(x, axis=-1, eps=1e-05):
    m = jnp.mean(x, axis=axis, keepdims=True)
    v = jnp.var(x, axis=axis, keepdims=True)
    return (x - m) / jnp.sqrt(v + eps)

def _scatter_add(tgt, idx, src, axis=0):
    return tgt.at[idx].add(src)

def _segment_sum(src, seg, n):
    return jax.ops.segment_sum(src, seg, n)
kernel_name = 'mk_xattn_seq_d1_seqx_r4_33b51e'

def setup_inputs(seed: int=0):
    np.random.seed(seed)
    _w = jnp.asarray

    def _rec_inputs():
        import jax
        import jax.numpy as jnp
        _rk = jax.random.key(seed)
        x = 7.22e-05 + 1 * jax.random.normal(jax.random.fold_in(_rk, 1), (8, 512, 512), jnp.float32)
        _lenS = 512 - jax.random.randint(jax.random.fold_in(_rk, 7), (8,), 0, max(1, 512 // 4) + 1, jnp.int32)
        _lenS2 = 1601 - jax.random.randint(jax.random.fold_in(_rk, 8), (8,), 0, max(1, 1601 // 4) + 1, jnp.int32)
        _ctx_2048P = jax.random.normal(jax.random.fold_in(_rk, 11), (8, 16, 512), jnp.float32)
        _ctx_2048c = jax.random.dirichlet(jax.random.fold_in(_rk, 511), 0.3 * jnp.ones((16,), jnp.float32), (8, 1601))
        _ctx_2048t = jnp.einsum('bsk,bkd->bsd', _ctx_2048c, _ctx_2048P)
        _ctx_2048t = _ctx_2048t * jax.lax.rsqrt(jnp.mean(jnp.square(_ctx_2048t)) + 1e-12) * 0.953939
        ctx_2048 = 3.03215e-05 + 0.0999827 * (_ctx_2048t + 0.3 * jax.random.normal(jax.random.fold_in(_rk, 611), (8, 1601, 512), jnp.float32))
        return (x, ctx_2048)
    x, ctx_2048 = _rec_inputs()

    def _L0_xattn_setup():
        import jax, jax.numpy as jnp
        import numpy as np
        N_HEAD = 32
        EPS = 1e-05

        def _ln(x, w, b):
            m = jnp.mean(x, axis=-1, keepdims=True)
            v = jnp.mean((x - m) ** 2, axis=-1, keepdims=True)
            return (x - m) * jax.lax.rsqrt(v + EPS) * w + b

        def _forward(x, state, i, ln1_w, ln1_b, ln2_w, ln2_b, maa_x, maa_w, maa_k, maa_v, maa_r, maa_g, maa_w1, maa_w2, time_decay, decay_w1, decay_w2, faaaa, Wr, Wk, Wv, Wg, Wo, gn_w, gn_b, fmaa_k, fmaa_r, fWk, fWr, fWv):
            B, L, C = x.shape
            H = N_HEAD
            S = C // H
            i0 = (2 + S) * i
            xa = _ln(x, ln1_w, ln1_b)
            sx = jnp.concatenate([state[:, i0 + 1][:, None], xa[:, :-1]], axis=1) - xa
            xxx = xa + sx * maa_x
            t = jnp.tanh(xxx @ maa_w1).reshape(B, L, 5, -1)
            m = jnp.einsum('blfd,fdc->blfc', t, maa_w2)
            mw, mk, mv, mr, mg = (m[:, :, j] for j in range(5))
            xw = xa + sx * (maa_w + mw)
            xk = xa + sx * (maa_k + mk)
            xv = xa + sx * (maa_v + mv)
            xr = xa + sx * (maa_r + mr)
            xg = xa + sx * (maa_g + mg)
            w = time_decay + jnp.tanh(xw @ decay_w1) @ decay_w2
            w = jnp.exp(-jnp.exp(w)).reshape(B, L, H, S)
            r = (xr @ Wr.T).reshape(B, L, H, S)
            k = (xk @ Wk.T).reshape(B, L, H, S)
            v = (xv @ Wv.T).reshape(B, L, H, S)
            g = jax.nn.silu(xg @ Wg.T)
            s0 = state[:, i0 + 2:i0 + 2 + S].reshape(B, H, S, S)

            def step(s, inp):
                k_l, v_l, w_l, r_l = inp
                a = k_l[..., :, None] * v_l[..., None, :]
                out = jnp.einsum('bhs,bhst->bht', r_l, faaaa * a + s)
                s_new = a + w_l[..., None] * s
                return (s_new, out)
            seq = tuple((z.transpose(1, 0, 2, 3) for z in (k, v, w, r)))
            _, outs = jax.lax.scan(step, s0, seq)
            y = outs.transpose(1, 0, 2, 3)
            gm = jnp.mean(y, axis=-1, keepdims=True)
            gv = jnp.mean((y - gm) ** 2, axis=-1, keepdims=True)
            y = ((y - gm) * jax.lax.rsqrt(gv + EPS)).reshape(B, L, C) * gn_w + gn_b
            x = x + y * g @ Wo.T
            xc = _ln(x, ln2_w, ln2_b)
            sxc = jnp.concatenate([state[:, i0][:, None], xc[:, :-1]], axis=1) - xc
            xk2 = xc + sxc * fmaa_k
            xr2 = xc + sxc * fmaa_r
            rr = jax.nn.sigmoid(xr2 @ fWr.T)
            kk = jnp.square(jax.nn.relu(xk2 @ fWk.T))
            x = x + rr * (kk @ fWv.T)
            return x
        key = jax.random.key(seed)
        B, L, C, H = (8, 128, 512, N_HEAD)
        S = C // H
        DM, DD = (32, 64)
        ks = jax.random.split(key, 32)
        n = lambda k, shp, s=1.0: jax.random.normal(k, shp, dtype=jnp.float32) * s
        u = lambda k, shp: jax.random.uniform(k, shp, dtype=jnp.float32)
        inp = {'x': n(ks[0], (B, L, C)), 'state': n(ks[1], (B, 2 + S, C), 0.1), 'i': 0, 'ln1_w': jnp.ones((C,), jnp.float32), 'ln1_b': jnp.zeros((C,), jnp.float32), 'ln2_w': jnp.ones((C,), jnp.float32), 'ln2_b': jnp.zeros((C,), jnp.float32), 'maa_x': u(ks[2], (C,)), 'maa_w': u(ks[3], (C,)), 'maa_k': u(ks[4], (C,)), 'maa_v': u(ks[5], (C,)), 'maa_r': u(ks[6], (C,)), 'maa_g': u(ks[7], (C,)), 'maa_w1': n(ks[8], (C, 5 * DM), 0.02), 'maa_w2': n(ks[9], (5, DM, C), 0.02), 'time_decay': n(ks[10], (C,), 0.5), 'decay_w1': n(ks[11], (C, DD), 0.02), 'decay_w2': n(ks[12], (DD, C), 0.02), 'faaaa': n(ks[13], (H, S, 1), 0.1), 'Wr': n(ks[14], (C, C), 0.02), 'Wk': n(ks[15], (C, C), 0.02), 'Wv': n(ks[16], (C, C), 0.02), 'Wg': n(ks[17], (C, C), 0.02), 'Wo': n(ks[18], (C, C), 0.02), 'gn_w': jnp.ones((C,), jnp.float32), 'gn_b': jnp.zeros((C,), jnp.float32), 'fmaa_k': u(ks[19], (C,)), 'fmaa_r': u(ks[20], (C,)), 'fWk': n(ks[21], (C, C), 0.02), 'fWr': n(ks[22], (C, C), 0.02), 'fWv': n(ks[23], (C, C), 0.02)}
        return inp
    _L0_xattn_all = _L0_xattn_setup()
    _L0_xattn_in = {k: v for k, v in _L0_xattn_all.items() if k in ('ln1_w', 'ln1_b', 'ln2_w', 'ln2_b', 'maa_x', 'maa_w', 'maa_k', 'maa_v', 'maa_r', 'maa_g', 'maa_w1', 'maa_w2', 'time_decay', 'decay_w1', 'decay_w2', 'faaaa', 'Wr', 'Wk', 'Wv', 'Wg', 'Wo', 'gn_w', 'gn_b', 'fmaa_k', 'fmaa_r', 'fWk', 'fWr', 'fWv')}
    del _L0_xattn_all
    return {'x': x, 'ctx_2048': ctx_2048, 'L0_xattn_ln1_w': _L0_xattn_in['ln1_w'], 'L0_xattn_ln1_b': _L0_xattn_in['ln1_b'], 'L0_xattn_ln2_w': _L0_xattn_in['ln2_w'], 'L0_xattn_ln2_b': _L0_xattn_in['ln2_b'], 'L0_xattn_maa_x': _L0_xattn_in['maa_x'], 'L0_xattn_maa_w': _L0_xattn_in['maa_w'], 'L0_xattn_maa_k': _L0_xattn_in['maa_k'], 'L0_xattn_maa_v': _L0_xattn_in['maa_v'], 'L0_xattn_maa_r': _L0_xattn_in['maa_r'], 'L0_xattn_maa_g': _L0_xattn_in['maa_g'], 'L0_xattn_maa_w1': _L0_xattn_in['maa_w1'], 'L0_xattn_maa_w2': _L0_xattn_in['maa_w2'], 'L0_xattn_time_decay': _L0_xattn_in['time_decay'], 'L0_xattn_decay_w1': _L0_xattn_in['decay_w1'], 'L0_xattn_decay_w2': _L0_xattn_in['decay_w2'], 'L0_xattn_faaaa': _L0_xattn_in['faaaa'], 'L0_xattn_Wr': _L0_xattn_in['Wr'], 'L0_xattn_Wk': _L0_xattn_in['Wk'], 'L0_xattn_Wv': _L0_xattn_in['Wv'], 'L0_xattn_Wg': _L0_xattn_in['Wg'], 'L0_xattn_Wo': _L0_xattn_in['Wo'], 'L0_xattn_gn_w': _L0_xattn_in['gn_w'], 'L0_xattn_gn_b': _L0_xattn_in['gn_b'], 'L0_xattn_fmaa_k': _L0_xattn_in['fmaa_k'], 'L0_xattn_fmaa_r': _L0_xattn_in['fmaa_r'], 'L0_xattn_fWk': _L0_xattn_in['fWk'], 'L0_xattn_fWr': _L0_xattn_in['fWr'], 'L0_xattn_fWv': _L0_xattn_in['fWv']}

def reference(x, ctx_2048, L0_xattn_ln1_w, L0_xattn_ln1_b, L0_xattn_ln2_w, L0_xattn_ln2_b, L0_xattn_maa_x, L0_xattn_maa_w, L0_xattn_maa_k, L0_xattn_maa_v, L0_xattn_maa_r, L0_xattn_maa_g, L0_xattn_maa_w1, L0_xattn_maa_w2, L0_xattn_time_decay, L0_xattn_decay_w1, L0_xattn_decay_w2, L0_xattn_faaaa, L0_xattn_Wr, L0_xattn_Wk, L0_xattn_Wv, L0_xattn_Wg, L0_xattn_Wo, L0_xattn_gn_w, L0_xattn_gn_b, L0_xattn_fmaa_k, L0_xattn_fmaa_r, L0_xattn_fWk, L0_xattn_fWr, L0_xattn_fWv):
    import jax
    import jax.numpy as jnp

    def _L0_xattn_ref(x, state, i, ln1_w, ln1_b, ln2_w, ln2_b, maa_x, maa_w, maa_k, maa_v, maa_r, maa_g, maa_w1, maa_w2, time_decay, decay_w1, decay_w2, faaaa, Wr, Wk, Wv, Wg, Wo, gn_w, gn_b, fmaa_k, fmaa_r, fWk, fWr, fWv):
        import jax, jax.numpy as jnp
        import numpy as np
        N_HEAD = 32
        EPS = 1e-05

        def _ln(x, w, b):
            m = jnp.mean(x, axis=-1, keepdims=True)
            v = jnp.mean((x - m) ** 2, axis=-1, keepdims=True)
            return (x - m) * jax.lax.rsqrt(v + EPS) * w + b

        def _forward(x, state, i, ln1_w, ln1_b, ln2_w, ln2_b, maa_x, maa_w, maa_k, maa_v, maa_r, maa_g, maa_w1, maa_w2, time_decay, decay_w1, decay_w2, faaaa, Wr, Wk, Wv, Wg, Wo, gn_w, gn_b, fmaa_k, fmaa_r, fWk, fWr, fWv):
            B, L, C = x.shape
            H = N_HEAD
            S = C // H
            i0 = (2 + S) * i
            xa = _ln(x, ln1_w, ln1_b)
            sx = jnp.concatenate([state[:, i0 + 1][:, None], xa[:, :-1]], axis=1) - xa
            xxx = xa + sx * maa_x
            t = jnp.tanh(xxx @ maa_w1).reshape(B, L, 5, -1)
            m = jnp.einsum('blfd,fdc->blfc', t, maa_w2)
            mw, mk, mv, mr, mg = (m[:, :, j] for j in range(5))
            xw = xa + sx * (maa_w + mw)
            xk = xa + sx * (maa_k + mk)
            xv = xa + sx * (maa_v + mv)
            xr = xa + sx * (maa_r + mr)
            xg = xa + sx * (maa_g + mg)
            w = time_decay + jnp.tanh(xw @ decay_w1) @ decay_w2
            w = jnp.exp(-jnp.exp(w)).reshape(B, L, H, S)
            r = (xr @ Wr.T).reshape(B, L, H, S)
            k = (xk @ Wk.T).reshape(B, L, H, S)
            v = (xv @ Wv.T).reshape(B, L, H, S)
            g = jax.nn.silu(xg @ Wg.T)
            s0 = state[:, i0 + 2:i0 + 2 + S].reshape(B, H, S, S)

            def step(s, inp):
                k_l, v_l, w_l, r_l = inp
                a = k_l[..., :, None] * v_l[..., None, :]
                out = jnp.einsum('bhs,bhst->bht', r_l, faaaa * a + s)
                s_new = a + w_l[..., None] * s
                return (s_new, out)
            seq = tuple((z.transpose(1, 0, 2, 3) for z in (k, v, w, r)))
            _, outs = jax.lax.scan(step, s0, seq)
            y = outs.transpose(1, 0, 2, 3)
            gm = jnp.mean(y, axis=-1, keepdims=True)
            gv = jnp.mean((y - gm) ** 2, axis=-1, keepdims=True)
            y = ((y - gm) * jax.lax.rsqrt(gv + EPS)).reshape(B, L, C) * gn_w + gn_b
            x = x + y * g @ Wo.T
            xc = _ln(x, ln2_w, ln2_b)
            sxc = jnp.concatenate([state[:, i0][:, None], xc[:, :-1]], axis=1) - xc
            xk2 = xc + sxc * fmaa_k
            xr2 = xc + sxc * fmaa_r
            rr = jax.nn.sigmoid(xr2 @ fWr.T)
            kk = jnp.square(jax.nn.relu(xk2 @ fWk.T))
            x = x + rr * (kk @ fWv.T)
            return x
        return _forward(x, state, i, ln1_w, ln1_b, ln2_w, ln2_b, maa_x, maa_w, maa_k, maa_v, maa_r, maa_g, maa_w1, maa_w2, time_decay, decay_w1, decay_w2, faaaa, Wr, Wk, Wv, Wg, Wo, gn_w, gn_b, fmaa_k, fmaa_r, fWk, fWr, fWv)
    x = _L0_xattn_ref(x, ctx_2048, 0, L0_xattn_ln1_w, L0_xattn_ln1_b, L0_xattn_ln2_w, L0_xattn_ln2_b, L0_xattn_maa_x, L0_xattn_maa_w, L0_xattn_maa_k, L0_xattn_maa_v, L0_xattn_maa_r, L0_xattn_maa_g, L0_xattn_maa_w1, L0_xattn_maa_w2, L0_xattn_time_decay, L0_xattn_decay_w1, L0_xattn_decay_w2, L0_xattn_faaaa, L0_xattn_Wr, L0_xattn_Wk, L0_xattn_Wv, L0_xattn_Wg, L0_xattn_Wo, L0_xattn_gn_w, L0_xattn_gn_b, L0_xattn_fmaa_k, L0_xattn_fmaa_r, L0_xattn_fWk, L0_xattn_fWr, L0_xattn_fWv)
    return x

_drawn_inputs = setup_inputs


def setup_inputs(seed=0):
    import zlib

    import numpy as np

    out = dict(_drawn_inputs(seed))
    spreads = {'L0_xattn_ln1_w': (1.0, 0.2),
     'L0_xattn_ln1_b': (0.0, 0.1),
     'L0_xattn_ln2_w': (1.0, 0.6),
     'L0_xattn_ln2_b': (0.0, 0.8),
     'L0_xattn_gn_w': (1.0, 0.6),
     'L0_xattn_gn_b': (0.0, 0.8)}
    factors = {'ctx_2048': 39.767,
     'L0_xattn_maa_x': 6.621,
     'L0_xattn_maa_w': 8.0,
     'L0_xattn_maa_w1': 3.404,
     'L0_xattn_maa_w2': 3.414,
     'L0_xattn_decay_w1': 8.0,
     'L0_xattn_decay_w2': 8.0,
     'L0_xattn_faaaa': 3.705,
     'L0_xattn_fmaa_r': 8.0,
     'L0_xattn_fWr': 7.499}
    for name, (base, spread) in spreads.items():
        noise = np.random.default_rng([zlib.crc32(name.encode()), seed]).standard_normal(out[name].shape)
        drawn = base * np.exp(spread * noise) if base else spread * noise
        out[name] = jnp.asarray(drawn.astype(out[name].dtype))
    for name, factor in factors.items():
        out[name] = (out[name] * factor).astype(out[name].dtype)
    return out
```

```python
from contextlib import ExitStack

import numpy as np

import concourse.bass as bass
from concourse import mybir

F32 = mybir.dt.float32
BF16 = mybir.dt.bfloat16
ALU = mybir.AluOpType
ACT = mybir.ActivationFunctionType

P = 128
BATCH, T, C = 8, 512, 512
HEAD = 16
EPS = 1e-5
G = C // P
TILES = T // P
HG = P // HEAD
J4 = 4
SLOTS = HEAD // 2
LORA = 32
DECAY = 64
KINDS = ("w", "k", "v", "r", "g")
VECS = ("ln1_w", "ln1_b", "ln2_w", "ln2_b", "maa_x", "maa_w", "maa_k", "maa_v", "maa_r", "maa_g",
        "time_decay", "faaaa", "gn_w", "gn_b", "fmaa_k", "fmaa_r")
BIG = ("Wv", "Wk", "Wr", "Wg", "Wo", "fWr", "fWk", "fWv")
SMALL = ("vecs", "lora1", "lora2", "lora2g", "dec1", "dec2", "ident", "sel_v", "sel_r", "ones",
         "avg", "center", "states", "s0")
MIX_ORDER = ("w", "v", "k", "r", "g")
MULS = len(KINDS) * G
STACK = 3 * J4 * 16
ACT_JOBS = 5 * G + 2 * G + 2 + 2 + TILES + G
DVE_JOBS = MULS + 2 * TILES
PROJECT_AT = {"v": 0, "k": 1, "w": 2, "r": 3, "g": 4}
PROJECT_LAST = {"v": 4, "k": 5, "w": 6, "r": 7, "g": 7}


class Banks:

    def __init__(self, banks, jobs_per_row):
        self.banks, self.jobs, self.n, self.loop = banks, jobs_per_row, 0, 0
        self.read = [None, None]

    def take(self, read_sem=None, value=None, per_row=None):
        at = self.n % 2
        self.n += 1
        free, self.read[at] = self.read[at], (read_sem, value, per_row)
        return self.banks[at], self.loop + self.n, free

    def enter(self, b):
        self.first, self.loop, self.kept = self.n, (b - 1) * self.jobs, list(self.read)
        if self.read[0]:
            self.read = [(sem, value + (b - 1) * per, per) if per is not None else None for sem, value, per in self.read]

    def leave(self):
        assert self.n - self.first == self.jobs and self.jobs % 2 == 0
        rows = BATCH - 2
        self.n, self.loop = self.first + rows * self.jobs, 0
        if self.kept[0] and self.kept[0][2] is not None:
            assert all(a[0] is k[0] for a, k in zip(self.read, self.kept))
            self.read = [(sem, value + rows * per, per) for sem, value, per in self.kept]


def wait(eng, sem, value):
    if isinstance(value, int) and value <= 0:
        return
    eng.wait_ge(sem, value)


def rows_done(b, ahead):
    return min(b + ahead + 1, BATCH) if isinstance(b, int) else b + ahead + 1


def build(nc, dram, out):
    with ExitStack() as ctx:
        def sb(name, shape, dt=F32):
            return ctx.enter_context(nc.sbuf_tensor(name, shape, dt))

        def psum(name):
            return ctx.enter_context(nc.psum_tensor(name, [P, T], F32))

        def sem(name):
            return ctx.enter_context(nc.semaphore(name))

        W = {n: sb(f"W_{n}", [P, G, C]) for n in BIG}
        small = {n: sb(f"c_{n}", dram[n].shape, dram[n].dtype) for n in SMALL}
        vecs = small["vecs"]
        eps, half = sb("eps", [P, 1]), sb("half", [P, 1])
        wait_carrier = sb("wait_carrier", [P, 1])
        half_gn = sb("half_gn", [P, 2, G])

        def vec(name, c):
            return vecs[:, VECS.index(name), c:c + 1]

        bufA = sb("bufA", [P, TILES, C])
        bufB = sb("bufB", [P, G, T + 1])
        bufD = sb("bufD", [P, G, T])
        x1 = sb("x1", [P, TILES, C])
        mixed = {k: sb(f"mixed_{k}", [P, G, T]) for k in "kvrg"}
        mixed["w"] = bufA
        xxx = mixed["g"]
        t4 = sb("t4", [P, T])
        tg = sb("tg", [LORA, T])
        td = sb("td", [DECAY, T])
        stats, mv, sd = ({n: sb(f"{name}{n}", shape) for n in (1, 2)} for name, shape in
                         (("stats", [P, TILES, 6]), ("mv", [P, TILES, 2]), ("sd", [P, TILES])))

        pk, pr, pv, pw, gate = (sb(n, [P, 2, T]) for n in ("pk", "pr", "pv", "pw", "gate"))
        act_tmp = sb("act_tmp", [P, T])
        v_hi, v_mid, v_lo = (sb(n, [P, T], BF16) for n in ("v_hi", "v_mid", "v_lo"))
        v_rest = sb("v_rest", [P, T])
        v_stack = sb("v_stack", [3 * 32, 2, J4, T], BF16)

        state = sb("state", [P, 2, 2, T + 1])
        diag = sb("diag", [P, T])
        fin_y = sb("fin_y", [P, T])
        fin_s = sb("fin_s", [P, T])
        yg = sb("yg", [P, G, T])

        ps_bc = [psum("ps_bc0"), psum("ps_bc1")]
        ps_y, ps_f = psum("ps_y"), psum("ps_f")
        ps_a = [psum("ps_a0"), psum("ps_a1")]
        ps_d = [psum("ps_d0"), psum("ps_d1")]

        big_in = {n: sem(f"{n}_in") for n in BIG}
        small_in, x_in, res_in, out_stored = sem("small_in"), sem("x_in"), sem("res_in"), sem("out_stored")
        stack_in = [sem("stack_in0"), sem("stack_in1")]
        consts_set = sem("consts_set")
        a_full, d_full = sem("a_full"), sem("d_full")
        bc_full, kv_set, s0_set, scan_set, rs_set, red_done = map(
            sem, ("bc_full", "kv_set", "s0_set", "scan_set", "rs_set", "red_done"))
        k_set, r_set, v_set, e_set, w_set, gp_set, th_set, gate_set = map(
            sem, ("k_set", "r_set", "v_set", "e_set", "w_set", "gp_set", "th_set", "gate_set"))
        vhi_set, vrest_set, vmid_set, vlo_set = map(sem, ("vhi_set", "vrest_set", "vmid_set", "vlo_set"))
        diag_set, diag_full, dv_set, y_set, cen_full, yc_set, sq_set, var_full = map(
            sem, ("diag_set", "diag_full", "dv_set", "y_set", "cen_full", "yc_set", "sq_set", "var_full"))
        gsd_set, grs_set, yn_set, z_set, yg_set = map(sem, ("gsd_set", "grs_set", "yn_set", "z_set", "yg_set"))
        ln_stats, ln_aggr, ln_sd, ln_rs, ln_norm, ln_out, ln_edge = (
            {n: sem(f"ln{n}_{name}") for n in (1, 2)}
            for name in ("stats", "aggr", "sd", "rs", "norm", "out", "edge"))
        sx_set, xxx_set, t_set, mul_set, mix_set, td_set = map(
            sem, ("sx_set", "xxx_set", "t_set", "mul_set", "mix_set", "td_set"))
        x1_set, sxc_set, xk_set, xr_set, rth_set, rr_set, relu_set, kk_set, rk_set, sum_set = map(
            sem, ("x1_set", "sxc_set", "xk_set", "xr_set", "rth_set", "rr_set", "relu_set", "kk_set", "rk_set",
                  "sum_set"))

        x_rows = dram["x"].rearrange("b (n p) c -> b p n c", p=P)
        out_rows = out.rearrange("b (n p) c -> b p n c", p=P)

        def stack_loaded(b, g):
            return STACK * (2 * b + g // 2 + 1)

        block = ctx.enter_context(nc.Block())

        @block.sync
        def _(sp):
            def load_x(b):
                if isinstance(b, int) and b < 2:
                    wait(sp, td_set, 2 * b)
                else:
                    wait(sp, relu_set, G * (b - 1))
                sp.dma_start(bufA[:, :, :], x_rows[b]).then_inc(x_in, 16)

            def load_residual(b):
                wait(sp, out_stored, 16 * TILES * b)
                sp.dma_start(x1[:, :, :], x_rows[b]).then_inc(res_in, 16)

            def stack(b, g):
                s = G * b + g
                for part, (src, ready) in enumerate(((v_hi, vhi_set), (v_mid, vmid_set), (v_lo, vlo_set))):
                    wait(sp, ready, s + 1)
                    for q in range(J4):
                        sp.dma_start(v_stack[32 * part:32 * part + 32, g % 2, q, :],
                                     src[32 * q:32 * q + 32, :]).then_inc(stack_in[g % 2], 16)

            def store(b):
                for n in range(TILES):
                    wait(sp, sum_set, TILES * b + n + 1)
                    sp.dma_start(out_rows[b, :, n, :], x1[:, n, :]).then_inc(out_stored, 16)

            def row(b, prev, more):
                stack(b, 1)
                stack(b, 2)
                if more:
                    load_x(b + 1)
                stack(b, 3)
                if prev:
                    store(b - 1)
                load_residual(b)
                if more:
                    stack(b + 1, 0)

            load_x(0)
            for n in SMALL:
                sp.dma_start(small[n][:], dram[n]).then_inc(small_in, 16)
            for n in BIG:
                sp.dma_start(W[n][:, :, :], dram[n]).then_inc(big_in[n], 16)
            stack(0, 0)
            row(0, False, True)
            with sp.Fori(1, BATCH - 1) as b:
                row(b, True, True)
            row(BATCH - 1, True, False)
            store(BATCH - 1)
            sp.wait_ge(out_stored, 16 * TILES * BATCH)

        @block.tensor
        def _(pe):
            a_banks, d_banks = Banks(ps_a, ACT_JOBS), Banks(ps_d, DVE_JOBS)

            def bank_of(banks, read_sem, value, per_row):
                dst, _, free = banks.take(read_sem, value, per_row)
                if free:
                    wait(pe, free[0], free[1])
                return dst

            def product(dst, lhs, rhs):
                for c in range(G):
                    last = nc.tensor.matmul(dst, lhs(c), rhs(c), start=(c == 0), stop=(c == G - 1))
                return last

            def transposes(n, b):
                pe.wait_ge(ln_norm[n], TILES * (b + 1))
                for c in range(G):
                    dst = bank_of(a_banks, ln_out[n], G * b + c + 1, G)
                    for t in range(TILES):
                        last = nc.tensor.transpose(dst[:, P * t:P * t + P], bufA[:, t, P * c:P * c + P],
                                                   small["ident"][:])
                    last.then_inc(a_full, 1)

            def low_rank(b):
                pe.wait_ge(xxx_set, G * (b + 1))
                dst = bank_of(a_banks, t_set, 2 * b + 1, 2)
                product(dst[:, :], lambda c: small["lora1"][:, c, 0:P], lambda c: xxx[:, c, :]).then_inc(a_full, 1)
                dst = bank_of(a_banks, t_set, 2 * b + 2, 2)
                product(dst[0:LORA, :], lambda c: small["lora1"][:, c, P:P + LORA],
                        lambda c: xxx[:, c, :]).then_inc(a_full, 1)

            def mixes(b, kind):
                f = KINDS.index(kind)
                pe.wait_ge(t_set, 2 * (b + 1))
                for c in range(G):
                    dst = bank_of(d_banks, mul_set, MULS * b + G * MIX_ORDER.index(kind) + c + 1, MULS)
                    if kind == "g":
                        lhs, rhs = small["lora2g"][:, P * c:P * c + P], tg[:, :]
                    else:
                        lhs, rhs = small["lora2"][LORA * f:LORA * f + LORA, P * c:P * c + P], t4[LORA * f:LORA * f + LORA, :]
                    nc.tensor.matmul(dst[:, :], lhs, rhs, start=True, stop=True).then_inc(d_full, 1)

            def decay(b):
                pe.wait_ge(mix_set, MULS * b + G)
                for h in range(2):
                    dst = bank_of(a_banks, td_set, 2 * b + h + 1, 2)
                    product(dst[0:DECAY, 0:T // 2], lambda c: small["dec1"][:, c, :],
                            lambda c: bufA[:, c, T // 2 * h:T // 2 * (h + 1)]).then_inc(a_full, 1)

            def project(b, g, kind):
                s = G * b + g
                cols = slice(P * g, P * g + P)
                read_sem = {"v": vhi_set, "k": k_set, "w": e_set, "r": r_set, "g": th_set}[kind]
                dst = bank_of(a_banks, read_sem, s + 1, G)
                if kind == "w":
                    pe.wait_ge(td_set, 2 * (b + 1))
                    last = nc.tensor.matmul(dst[:, :], small["dec2"][:, cols], td[:, :], start=True, stop=True)
                else:
                    pe.wait_ge(mix_set, MULS * b + G * (MIX_ORDER.index(kind) + 1))
                    w = W["W" + kind]
                    last = product(dst[:, :], lambda c: w[:, c, cols], lambda c: mixed[kind][:, c, :])
                last.then_inc(a_full, 1)

            def broadcast(b, g, j):
                wait(pe, kv_set, (G * b + g) * HEAD + j - 1)
                nc.tensor.matmul(ps_bc[j % 2][:, :], small["sel_v"][:, j % J4, :],
                                 v_stack[:, g % 2, j // J4, :], start=True, stop=True).then_inc(bc_full, 1)

            def reduce(b, g, i):
                s = G * b + g
                pe.wait_ge(rs_set, SLOTS * s + i + 1)
                if i == 0:
                    wait(pe, y_set, s)
                for e in range(2):
                    j = 2 * i + e
                    q = j // J4
                    last = nc.tensor.matmul(ps_y[32 * q:32 * q + 32, :], small["sel_r"][:, j % J4, :],
                                            state[:, i % 2, e, 0:T], start=(j % J4 == 0), stop=(j % J4 == J4 - 1))
                last.then_inc(red_done, 1)

            def diagonal(s):
                pe.wait_ge(diag_set, s + 1)
                wait(pe, gsd_set, s)
                nc.tensor.matmul(ps_f[:, :], small["ones"][:], diag[:, :], start=True, stop=True).then_inc(diag_full, 1)

            def centre(s):
                pe.wait_ge(y_set, s + 1)
                nc.tensor.matmul(ps_f[:, :], small["center"][:], fin_y[:, :], start=True, stop=True).then_inc(cen_full, 1)

            def variance(s):
                pe.wait_ge(sq_set, s + 1)
                nc.tensor.matmul(ps_f[:, :], small["avg"][:], fin_s[:, :], start=True, stop=True).then_inc(var_full, 1)

            def out_proj(b, t):
                dst = bank_of(d_banks, x1_set, TILES * b + t + 1, TILES)
                pe.wait_ge(yg_set, G * (b + 1))
                product(dst[:, :], lambda c: yg[:, c, P * t:P * t + P], lambda c: W["Wo"][:, c, :]).then_inc(d_full, 1)

            def receptance(b, t):
                dst = bank_of(a_banks, rth_set, TILES * b + t + 1, TILES)
                pe.wait_ge(xr_set, G * (b + 1))
                product(dst[:, :], lambda c: bufD[:, c, P * t:P * t + P], lambda c: W["fWr"][:, c, :]).then_inc(a_full, 1)

            def key(b, f):
                dst = bank_of(a_banks, relu_set, G * b + f + 1, G)
                pe.wait_ge(xk_set, G * (b + 1))
                product(dst[:, :], lambda c: W["fWk"][:, c, P * f:P * f + P], lambda c: bufA[:, c, :]).then_inc(a_full, 1)

            def value(b, t):
                dst = bank_of(d_banks, rk_set, TILES * b + t + 1, TILES)
                pe.wait_ge(kk_set, G * (b + 1))
                product(dst[:, :], lambda c: bufD[:, c, P * t:P * t + P], lambda c: W["fWv"][:, c, :]).then_inc(d_full, 1)

            def row(b, prev, more):
                for g in range(G):
                    s = G * b + g
                    for i in range(SLOTS):
                        if i == 0:
                            pe.wait_ge(stack_in[g % 2], stack_loaded(b, g))
                        broadcast(b, g, 2 * i)
                        broadcast(b, g, 2 * i + 1)
                        if i > 0:
                            reduce(b, g, i - 1)
                        elif g > 0:
                            reduce(b, g - 1, SLOTS - 1)
                        elif prev:
                            reduce(b - 1, G - 1, SLOTS - 1)
                        if (g > 0 or prev) and i == 1:
                            centre(s - 1)
                        if g < G - 1:
                            for kind in [k for k, at in PROJECT_AT.items() if at == i]:
                                project(b, g + 1, kind)
                        elif more:
                            for kind in [k for k, at in PROJECT_LAST.items() if at == i]:
                                project(b + 1, 0, kind)
                        if (g > 0 or prev) and i == 2:
                            variance(s - 1)
                        if i == 6:
                            diagonal(s)
                        if prev and g == 0 and i >= 5:
                            for t in ((0,), (1,), (2, 3))[i - 5]:
                                out_proj(b - 1, t)
                        if prev and g == 1 and i == 1:
                            transposes(2, b - 1)
                        if prev and g == 1 and i in (4, 5):
                            receptance(b - 1, 2 * (i - 4))
                            receptance(b - 1, 2 * (i - 4) + 1)
                        if prev and g == 1 and i in (6, 7):
                            key(b - 1, 2 * (i - 6))
                            key(b - 1, 2 * (i - 6) + 1)
                        if prev and g == 2 and i < TILES:
                            value(b - 1, i)
                        if more and g == 2 and i == 4:
                            transposes(1, b + 1)
                        if more and g == 2 and i == 6:
                            low_rank(b + 1)
                        if more and g == 2 and i == 7:
                            mixes(b + 1, "w")
                        if more and g == 3 and i < 4:
                            mixes(b + 1, MIX_ORDER[i + 1])
                        if more and g == 3 and i == 1:
                            decay(b + 1)

            pe.wait_ge(small_in, 16 * len(SMALL))
            transposes(1, 0)
            low_rank(0)
            mixes(0, "w")
            mixes(0, "v")
            mixes(0, "k")
            decay(0)
            mixes(0, "r")
            mixes(0, "g")
            for kind in PROJECT_LAST:
                if kind != "w":
                    pe.wait_ge(big_in["W" + kind], 16)
                project(0, 0, kind)
            row(0, False, True)
            for n in ("Wo", "fWr", "fWk", "fWv"):
                pe.wait_ge(big_in[n], 16)
            with pe.Fori(1, BATCH - 1) as b:
                a_banks.enter(b)
                d_banks.enter(b)
                row(b, True, True)
            a_banks.leave()
            d_banks.leave()
            last = BATCH - 1
            row(last, True, False)
            reduce(last, G - 1, SLOTS - 1)
            centre(G * BATCH - 1)
            variance(G * BATCH - 1)
            for t in range(TILES):
                out_proj(last, t)
            transposes(2, last)
            for t in range(TILES):
                receptance(last, t)
            for f in range(G):
                key(last, f)
            for t in range(TILES):
                value(last, t)

        @block.scalar
        def _(act):
            banks = Banks(ps_a, ACT_JOBS)

            def job():
                src, number, _ = banks.take()
                act.wait_ge(a_full, number)
                return src

            def norm_sd(n, b):
                act.wait_ge(ln_aggr[n], TILES * (b + 1))
                nc.scalar.activation(sd[n][:, :], mv[n][:, :, 1], ACT.Sqrt, bias=eps[:, :]).then_inc(ln_sd[n], 1)

            def norm_out(n, b):
                if n == 1:
                    wait(act, mix_set, MULS * b)
                    wait(act, sum_set, TILES * (b - 1))
                else:
                    act.wait_ge(mix_set, MULS * rows_done(b, 1))
                for c in range(G):
                    src = job()
                    nc.scalar.activation(bufB[:, c, 1:T + 1], src[:, :], ACT.Identity, bias=vec(f"ln{n}_b", c),
                                         scale=vec(f"ln{n}_w", c)).then_inc(ln_out[n], 1)

            def low_rank(b):
                wait(act, mul_set, MULS * b)
                nc.scalar.activation(t4[:, :], job()[:, :], ACT.Tanh).then_inc(t_set, 1)
                nc.scalar.activation(tg[:, :], job()[0:LORA, :], ACT.Tanh).then_inc(t_set, 1)

            def decay(b):
                wait(act, e_set, G * b)
                for h in range(2):
                    nc.scalar.activation(td[:, T // 2 * h:T // 2 * (h + 1)], job()[0:DECAY, 0:T // 2],
                                         ACT.Tanh).then_inc(td_set, 1)

            def project(b, g, kind):
                s, par = G * b + g, g % 2
                src = job()
                if kind == "v":
                    wait(act, dv_set, s - 1)
                    nc.scalar.activation(pv[:, par, :], src[:, :], ACT.Copy).then_inc(v_set, 1)
                    wait(act, bc_full, HEAD * (s - 1))
                    if isinstance(s, int) and s == 0:
                        pass
                    elif g > 0:
                        act.wait_ge(stack_in[(g - 1) % 2], stack_loaded(b, g - 1))
                    else:
                        act.wait_ge(stack_in[1], stack_loaded(b - 1, G - 1))
                    nc.scalar.activation(v_hi[:, :], src[:, :], ACT.Copy).then_inc(vhi_set, 1)
                elif kind == "k":
                    wait(act, kv_set, HEAD * (s - 1))
                    wait(act, diag_set, s - 1)
                    nc.scalar.activation(pk[:, par, :], src[:, :], ACT.Copy).then_inc(k_set, 1)
                elif kind == "r":
                    wait(act, rs_set, SLOTS * (s - 1))
                    wait(act, diag_set, s - 1)
                    nc.scalar.activation(pr[:, par, :], src[:, :], ACT.Copy).then_inc(r_set, 1)
                elif kind == "w":
                    wait(act, gate_set, s)
                    nc.scalar.activation(act_tmp[:, :], src[:, :], ACT.Exp, bias=vec("time_decay", g)).then_inc(e_set, 1)
                    act.wait_ge(e_set, s + 1)
                    wait(act, scan_set, HEAD * (s - 1))
                    nc.scalar.activation(pw[:, par, :], act_tmp[:, :], ACT.Exp, scale=-1.0).then_inc(w_set, 1)
                else:
                    wait(act, yg_set, s - 1)
                    nc.scalar.activation(gate[:, par, :], src[:, :], ACT.Copy).then_inc(gp_set, 1)
                    act.wait_ge(w_set, s + 1)
                    nc.scalar.activation(act_tmp[:, :], src[:, :], ACT.Tanh, scale=0.5).then_inc(th_set, 1)

            def v_middle(s):
                act.wait_ge(vrest_set, s + 1)
                nc.scalar.activation(v_mid[:, :], v_rest[:, :], ACT.Copy).then_inc(vmid_set, 1)

            def centred(s):
                act.wait_ge(cen_full, s + 1)
                nc.scalar.activation(fin_y[:, :], ps_f[:, :], ACT.Copy).then_inc(yc_set, 1)
                wait(act, yn_set, s)
                nc.scalar.activation(fin_s[:, :], ps_f[:, :], ACT.Square).then_inc(sq_set, 1)

            def group_sd(s):
                act.wait_ge(var_full, s + 1)
                nc.scalar.activation(fin_s[:, :], ps_f[:, :], ACT.Sqrt, bias=eps[:, :]).then_inc(gsd_set, 1)

            def group_affine(s, g):
                act.wait_ge(yn_set, s + 1)
                nc.scalar.activation(fin_y[:, :], fin_y[:, :], ACT.Identity, bias=half_gn[:, 1, g:g + 1],
                                     scale=half_gn[:, 0, g:g + 1]).then_inc(z_set, 1)

            def receptance(b, t):
                nc.scalar.activation(bufB[:, t, 0:T], job()[:, :], ACT.Tanh, scale=0.5).then_inc(rth_set, 1)
                act.wait_ge(rth_set, TILES * b + t + 1)
                nc.scalar.activation(bufB[:, t, 0:T], bufB[:, t, 0:T], ACT.Identity, bias=half[:, :],
                                     scale=0.5).then_inc(rr_set, 1)

            def key(b, f):
                if f == 0:
                    act.wait_ge(rth_set, TILES * (b + 1))
                nc.scalar.activation(bufD[:, f, :], job()[:, :], ACT.Relu).then_inc(relu_set, 1)

            def row(b, prev, more):
                for g in range(G):
                    s = G * b + g
                    for i in range(SLOTS):
                        if (g > 0 or prev) and i == 1:
                            centred(s - 1)
                        if (g > 0 or prev) and i == 4:
                            group_affine(s - 1, (g - 1) % G)
                        if g < G - 1:
                            for kind in [k for k, at in PROJECT_AT.items() if at == i]:
                                project(b, g + 1, kind)
                            if i == PROJECT_AT["v"] + 1:
                                v_middle(s + 1)
                        elif more:
                            for kind in [k for k, at in PROJECT_LAST.items() if at == i]:
                                project(b + 1, 0, kind)
                            if i == PROJECT_LAST["v"] + 1:
                                v_middle(s + 1)
                        if (g > 0 or prev) and i == 2:
                            group_sd(s - 1)
                        if prev and g == 1 and i == 0:
                            norm_sd(2, b - 1)
                        if prev and g == 1 and i == 1:
                            norm_out(2, b - 1)
                        if prev and g == 1 and i in (4, 5):
                            receptance(b - 1, 2 * (i - 4))
                            receptance(b - 1, 2 * (i - 4) + 1)
                        if prev and g == 1 and i in (6, 7):
                            key(b - 1, 2 * (i - 6))
                            key(b - 1, 2 * (i - 6) + 1)
                        if more and g == 2 and i == 3:
                            norm_sd(1, b + 1)
                        if more and g == 2 and i == 4:
                            norm_out(1, b + 1)
                        if more and g == 2 and i == 6:
                            low_rank(b + 1)
                        if more and g == 3 and i == 1:
                            decay(b + 1)

            act.wait_ge(small_in, 16 * len(SMALL))
            act.wait_ge(consts_set, 3)
            norm_sd(1, 0)
            norm_out(1, 0)
            low_rank(0)
            decay(0)
            for kind in PROJECT_LAST:
                project(0, 0, kind)
                if kind == "v":
                    v_middle(0)
            row(0, False, True)
            with act.Fori(1, BATCH - 1) as b:
                banks.enter(b)
                row(b, True, True)
            banks.leave()
            last = BATCH - 1
            row(last, True, False)
            centred(G * BATCH - 1)
            group_sd(G * BATCH - 1)
            group_affine(G * BATCH - 1, G - 1)
            norm_sd(2, last)
            norm_out(2, last)
            for t in range(TILES):
                receptance(last, t)
            for f in range(G):
                key(last, f)

        @block.vector
        def _(dve):
            banks = Banks(ps_d, DVE_JOBS)

            def job():
                src, number, _ = banks.take()
                dve.wait_ge(d_full, number)
                return src

            def pair(b, g, i):
                s, par, two = G * b + g, g % 2, state[:, i % 2]
                if i == 0:
                    dve.wait_ge(k_set, s + 1)
                wait(dve, red_done, SLOTS * s + i - 1)
                nc.vector.tensor_copy(two[:, :, 0], small["s0"][:, b, g, 2 * i:2 * i + 2]).then_inc(s0_set, 1)
                for e in range(2):
                    dve.wait_ge(bc_full, HEAD * s + 2 * i + e + 1)
                    nc.vector.tensor_tensor(two[:, e, 1:T + 1], ps_bc[e][:, :], pk[:, par, :], ALU.mult)\
                        .then_inc(kv_set, 1)
                if i == 0:
                    dve.wait_ge(w_set, s + 1)
                dve.wait_ge(s0_set, SLOTS * s + i + 1)
                for e in range(2):
                    dve.wait_ge(kv_set, HEAD * s + 2 * i + e + 1)
                    nc.vector.tensor_tensor_scan(two[:, e, 1:T + 1], pw[:, par, :], two[:, e, 1:T + 1],
                                                 two[:, e, 0:1], ALU.mult, ALU.add).then_inc(scan_set, 1)

            def diagonal(b, g):
                s, par = G * b + g, g % 2
                dve.wait_ge(r_set, s + 1)
                wait(dve, y_set, s)
                nc.vector.scalar_tensor_tensor(diag[:, :], pr[:, par, :], vec("faaaa", g), pk[:, par, :],
                                               ALU.mult, ALU.mult).then_inc(diag_set, 1)

            def diagonal_v(b, g):
                s = G * b + g
                dve.wait_ge(diag_full, s + 1)
                dve.wait_ge(v_set, s + 1)
                nc.vector.tensor_tensor(diag[:, :], ps_f[:, :], pv[:, g % 2, :], ALU.mult).then_inc(dv_set, 1)

            def sum_y(s):
                dve.wait_ge(red_done, SLOTS * (s + 1))
                dve.wait_ge(dv_set, s + 1)
                wait(dve, yg_set, s)
                nc.vector.tensor_tensor(fin_y[:, :], ps_y[:, :], diag[:, :], ALU.add).then_inc(y_set, 1)

            def group_rs(s):
                dve.wait_ge(gsd_set, s + 1)
                nc.vector.reciprocal(fin_s[:, :], fin_s[:, :]).then_inc(grs_set, 1)

            def gate_silu(b, g):
                dve.wait_ge(th_set, G * b + g + 1)
                nc.vector.scalar_tensor_tensor(gate[:, g % 2, :], act_tmp[:, :], 1.0, gate[:, g % 2, :],
                                               ALU.add, ALU.mult).then_inc(gate_set, 1)

            def norm_stats(n, src, b, t):
                nc.vector.bn_stats(stats[n][:, t, :], src[:, t, :]).then_inc(ln_stats[n], 1)

            def norm_aggr(n, b):
                dve.wait_ge(ln_stats[n], TILES * (b + 1))
                nc.vector.memset(wait_carrier[:, :], 0.0)
                for t in range(TILES):
                    nc.vector.bn_aggr(mv[n][:, t, :], stats[n][:, t, :]).then_inc(ln_aggr[n], 1)

            def norm(n, src, b):
                dve.wait_ge(ln_sd[n], b + 1)
                nc.vector.reciprocal(sd[n][:, :], sd[n][:, :]).then_inc(ln_rs[n], 1)
                dve.wait_ge(ln_rs[n], b + 1)
                if n == 2:
                    dve.wait_ge(td_set, 2 * rows_done(b, 1))
                for t in range(TILES):
                    nc.vector.tensor_scalar(bufA[:, t, :], src[:, t, :], mv[n][:, t, 0:1], sd[n][:, t:t + 1],
                                            ALU.subtract, ALU.mult).then_inc(ln_norm[n], 1)

            def low_rank_in(b):
                wait(dve, th_set, G * b)
                for c in range(G):
                    dve.wait_ge(sx_set, G * b + c + 1)
                    nc.vector.scalar_tensor_tensor(xxx[:, c, :], bufD[:, c, :], vec("maa_x", c), bufB[:, c, 1:T + 1],
                                                   ALU.mult, ALU.add).then_inc(xxx_set, 1)

            def mixes(b, kind):
                if kind == "w":
                    dve.wait_ge(ln_out[1], G * (b + 1))
                elif kind == "g":
                    dve.wait_ge(t_set, 2 * (b + 1))
                else:
                    wait(dve, {"v": vhi_set, "k": k_set, "r": r_set}[kind], G * b)
                for c in range(G):
                    src = job()
                    nc.vector.scalar_tensor_tensor(mixed[kind][:, c, :], src[:, :], vec(f"maa_{kind}", c), bufD[:, c, :],
                                                   ALU.add, ALU.mult).then_inc(mul_set, 1)

            def residual(b, t):
                if t == 0:
                    dve.wait_ge(res_in, 16 * (b + 1))
                src = job()
                nc.vector.tensor_tensor(x1[:, t, :], src[:, :], x1[:, t, :], ALU.add).then_inc(x1_set, 1)
                dve.wait_ge(x1_set, TILES * b + t + 1)
                norm_stats(2, x1, b, t)

            def channel_mix(b, name, into, done):
                for c in range(G):
                    if name == "fmaa_k":
                        dve.wait_ge(sxc_set, G * b + c + 1)
                    nc.vector.scalar_tensor_tensor(into[:, c, :], bufD[:, c, :], vec(name, c), bufB[:, c, 1:T + 1],
                                                   ALU.mult, ALU.add).then_inc(done, 1)

            def key_mix(b):
                dve.wait_ge(ln_out[2], G * (b + 1))
                channel_mix(b, "fmaa_k", bufA, xk_set)

            def receptance_mix(b):
                dve.wait_ge(xk_set, G * (b + 1))
                channel_mix(b, "fmaa_r", bufD, xr_set)

            def value(b, t):
                dve.wait_ge(rr_set, TILES * b + t + 1)
                src = job()
                nc.vector.tensor_tensor(bufB[:, t, 0:T], src[:, :], bufB[:, t, 0:T], ALU.mult).then_inc(rk_set, 1)

            def row(b, prev, more):
                for g in range(G):
                    s = G * b + g
                    for i in range(SLOTS):
                        pair(b, g, i)
                        if (g > 0 or prev) and i == 0:
                            sum_y(s - 1)
                        if (g > 0 or prev) and i == 3:
                            group_rs(s - 1)
                        if i == 5:
                            diagonal(b, g)
                        if i == 7:
                            diagonal_v(b, g)
                        if g < G - 1 and i == PROJECT_AT["g"] + 1:
                            gate_silu(b, g + 1)
                        if g == G - 1 and more and i == PROJECT_LAST["g"]:
                            gate_silu(b + 1, 0)
                        if prev and g == 0 and i >= 5:
                            for t in ((0,), (1,), (2, 3))[i - 5]:
                                residual(b - 1, t)
                        if prev and g == 1 and i == 0:
                            norm_aggr(2, b - 1)
                            norm(2, x1, b - 1)
                        if prev and g == 1 and i == 2:
                            key_mix(b - 1)
                        if prev and g == 1 and i == 3:
                            receptance_mix(b - 1)
                        if prev and g == 2 and i < TILES:
                            value(b - 1, i)
                        if more and g == 2 and i == 3:
                            dve.wait_ge(x_in, 16 * (b + 2))
                            for t in range(TILES):
                                norm_stats(1, bufA, b + 1, t)
                            norm_aggr(1, b + 1)
                        if more and g == 2 and i == 4:
                            norm(1, bufA, b + 1)
                        if more and g == 2 and i == 5:
                            low_rank_in(b + 1)
                        if more and g == 2 and i == 7:
                            mixes(b + 1, "w")
                        if more and g == 3 and i < 4:
                            mixes(b + 1, MIX_ORDER[i + 1])

            nc.vector.memset(eps[:, :], EPS).then_inc(consts_set, 1)
            nc.vector.memset(half[:, :], 0.5).then_inc(consts_set, 1)
            dve.wait_ge(small_in, 16 * len(SMALL))
            n = VECS.index("gn_w")
            nc.vector.tensor_scalar(half_gn[:, :, :], vecs[:, n:n + 2, :], 0.5, None, ALU.mult).then_inc(consts_set, 1)
            dve.wait_ge(x_in, 16)
            for t in range(TILES):
                norm_stats(1, bufA, 0, t)
            norm_aggr(1, 0)
            norm(1, bufA, 0)
            low_rank_in(0)
            for kind in MIX_ORDER:
                mixes(0, kind)
            gate_silu(0, 0)
            row(0, False, True)
            with dve.Fori(1, BATCH - 1) as b:
                banks.enter(b)
                row(b, True, True)
            banks.leave()
            last = BATCH - 1
            row(last, True, False)
            sum_y(G * BATCH - 1)
            group_rs(G * BATCH - 1)
            for t in range(TILES):
                residual(last, t)
            norm_aggr(2, last)
            norm(2, x1, last)
            key_mix(last)
            receptance_mix(last)
            for t in range(TILES):
                value(last, t)

        @block.gpsimd
        def _(pool):
            def read_out(b, g, i):
                s = G * b + g
                if i == 0:
                    pool.wait_ge(r_set, s + 1)
                pool.wait_ge(scan_set, HEAD * s + 2 * i + 2)
                nc.gpsimd.tensor_tensor(state[:, i % 2, :, 0:T], state[:, i % 2, :, 0:T],
                                        pr[:, g % 2, :].unsqueeze(1).to_broadcast([P, 2, T]), ALU.mult)\
                    .then_inc(rs_set, 1)

            def v_parts(b, g):
                s = G * b + g
                pool.wait_ge(vhi_set, s + 1)
                wait(pool, vlo_set, s)
                nc.gpsimd.tensor_tensor(v_rest[:, :], pv[:, g % 2, :], v_hi[:, :], ALU.subtract).then_inc(vrest_set, 1)
                pool.wait_ge(vmid_set, s + 1)
                nc.gpsimd.tensor_tensor(v_lo[:, :], v_rest[:, :], v_mid[:, :], ALU.subtract).then_inc(vlo_set, 1)

            def normalise_y(s):
                pool.wait_ge(grs_set, s + 1)
                nc.gpsimd.tensor_tensor(fin_y[:, :], fin_y[:, :], fin_s[:, :], ALU.mult).then_inc(yn_set, 1)

            def gated_y(b, g):
                s = G * b + g
                pool.wait_ge(z_set, s + 1)
                pool.wait_ge(gate_set, s + 1)
                if g == 0:
                    wait(pool, x1_set, TILES * b)
                nc.gpsimd.tensor_tensor(yg[:, g, :], fin_y[:, :], gate[:, g % 2, :], ALU.mult).then_inc(yg_set, 1)

            def edge(n, b):
                if n == 1:
                    wait(pool, mix_set, MULS * b)
                    wait(pool, sum_set, TILES * (b - 1))
                else:
                    pool.wait_ge(mix_set, MULS * rows_done(b, 1))
                nc.gpsimd.tensor_copy(bufB[:, :, 0], small["states"][:, b, n - 1, :]).then_inc(ln_edge[n], 1)

            def shift(n, b, done):
                pool.wait_ge(ln_edge[n], b + 1)
                if n == 1:
                    wait(pool, rk_set, TILES * (b - 1))
                    wait(pool, mul_set, MULS * b)
                else:
                    pool.wait_ge(mul_set, MULS * rows_done(b, 1))
                for c in range(G):
                    pool.wait_ge(ln_out[n], G * b + c + 1)
                    nc.gpsimd.tensor_tensor(bufD[:, c, :], bufB[:, c, 0:T], bufB[:, c, 1:T + 1], ALU.subtract)\
                        .then_inc(done, 1)

            def mixes(b, kind):
                for c in range(G):
                    pool.wait_ge(mul_set, MULS * b + G * MIX_ORDER.index(kind) + c + 1)
                    nc.gpsimd.tensor_tensor(mixed[kind][:, c, :], mixed[kind][:, c, :], bufB[:, c, 1:T + 1], ALU.add)\
                        .then_inc(mix_set, 1)

            def square(b, f):
                pool.wait_ge(relu_set, G * b + f + 1)
                nc.gpsimd.tensor_tensor(bufD[:, f, :], bufD[:, f, :], bufD[:, f, :], ALU.mult).then_inc(kk_set, 1)

            def total(b, t):
                pool.wait_ge(rk_set, TILES * b + t + 1)
                nc.gpsimd.tensor_tensor(x1[:, t, :], x1[:, t, :], bufB[:, t, 0:T], ALU.add).then_inc(sum_set, 1)

            def row(b, prev, more):
                for g in range(G):
                    s = G * b + g
                    for i in range(SLOTS):
                        read_out(b, g, i)
                        if g < G - 1 and i == PROJECT_AT["v"]:
                            v_parts(b, g + 1)
                        if g == G - 1 and more and i == PROJECT_LAST["v"]:
                            v_parts(b + 1, 0)
                        if (g > 0 or prev) and i == 3:
                            normalise_y(s - 1)
                        if i == 4 and g > 0:
                            gated_y(b, g - 1)
                        if i == 4 and g == 0 and prev:
                            gated_y(b - 1, G - 1)
                        if prev and g == 1 and i == 1:
                            edge(2, b - 1)
                            shift(2, b - 1, sxc_set)
                        if prev and g == 1 and i in (6, 7):
                            square(b - 1, 2 * (i - 6))
                            square(b - 1, 2 * (i - 6) + 1)
                        if prev and g == 2 and i < TILES:
                            total(b - 1, i)
                        if more and g == 2 and i == 4:
                            edge(1, b + 1)
                            shift(1, b + 1, sx_set)
                        if more and g == 2 and i == 7:
                            mixes(b + 1, "w")
                        if more and g == 3 and i < 4:
                            mixes(b + 1, MIX_ORDER[i + 1])

            pool.wait_ge(small_in, 16 * len(SMALL))
            edge(1, 0)
            shift(1, 0, sx_set)
            for kind in MIX_ORDER:
                mixes(0, kind)
            v_parts(0, 0)
            row(0, False, True)
            with pool.Fori(1, BATCH - 1) as b:
                row(b, True, True)
            last = BATCH - 1
            row(last, True, False)
            normalise_y(G * BATCH - 1)
            gated_y(last, G - 1)
            edge(2, last)
            shift(2, last, sxc_set)
            for f in range(G):
                square(last, f)
            for t in range(TILES):
                total(last, t)


def kernel(**inputs):
    import ml_dtypes
    import concourse.bacc as bacc
    from concourse.bass_utils import run_bass_kernel_spmd

    a = {k.replace("L0_xattn_", ""): np.asarray(v) for k, v in inputs.items()}
    jh = np.arange(C).reshape(G, HG, HEAD).transpose(0, 2, 1).reshape(C)

    def chunks(w):
        return np.ascontiguousarray(w.reshape(-1, P, w.shape[1]).transpose(1, 0, 2))

    def channel_major(v):
        v = v.reshape(v.shape[:-1] + (G, P))
        return np.moveaxis(v, -1, 0)

    vectors = dict(a, faaaa=a["faaaa"].reshape(C), gn_w=a["gn_w"][jh], gn_b=a["gn_b"][jh])
    ctx_rows = a["ctx_2048"]
    eye, row, col = np.eye(P, dtype=np.float32), np.arange(P)[:, None], np.arange(P)[None, :]
    same_head = (row % HG == col % HG).astype(np.float32)
    arrays = {
        "x": a["x"],
        "vecs": np.stack([channel_major(vectors[n]) for n in VECS], axis=1),
        "lora1": chunks(a["maa_w1"]),
        "lora2": a["maa_w2"][:4].reshape(4 * LORA, C),
        "lora2g": a["maa_w2"][4],
        "dec1": chunks(a["decay_w1"]),
        "dec2": a["decay_w2"],
        "ident": eye,
        "sel_v": np.stack([((np.arange(96)[:, None] % 32) == HG * jj + col // HEAD) for jj in range(J4)], axis=1)
        .astype(ml_dtypes.bfloat16),
        "sel_r": np.stack([(np.arange(32)[None, :] == HG * jj + row // HEAD) for jj in range(J4)], axis=1)
        .astype(np.float32),
        "ones": (row // HEAD == col % HG).astype(np.float32),
        "avg": same_head / HEAD,
        "center": eye - same_head / HEAD,
        "states": channel_major(ctx_rows[:, [1, 0]]),
        "s0": ctx_rows[:, 2:2 + HEAD].reshape(BATCH, G, P, HEAD).transpose(2, 0, 1, 3),
        "Wv": chunks(a["Wv"].T[:, jh]), "Wg": chunks(a["Wg"].T[:, jh]),
        "Wk": chunks(a["Wk"].T), "Wr": chunks(a["Wr"].T), "Wo": chunks(a["Wo"].T[jh]),
        "fWr": chunks(a["fWr"].T), "fWk": chunks(a["fWk"].T), "fWv": chunks(a["fWv"].T),
    }
    arrays = {k: np.ascontiguousarray(v) for k, v in arrays.items()}
    nc = bacc.Bacc("TRN2", target_bir_lowering=False, num_devices=1)
    dram = {n: nc.dram_tensor(f"in_{n}", v.shape, mybir.dt.from_np(v.dtype), kind="ExternalInput").ap()
            for n, v in arrays.items()}
    out = nc.dram_tensor("out_0", (BATCH, T, C), F32, kind="ExternalOutput").ap()
    build(nc, dram, out)
    r = run_bass_kernel_spmd(nc, [{f"in_{n}": v for n, v in arrays.items()}], core_ids=[0])
    return r.results[0]["out_0"]
```

```python
from contextlib import ExitStack

import numpy as np

import concourse.bass as bass
from concourse import mybir

F32 = mybir.dt.float32
BF16 = mybir.dt.bfloat16
ALU = mybir.AluOpType
ACT = mybir.ActivationFunctionType

P = 128
BATCH, T, C = 8, 512, 512
HEAD = 16
EPS = 1e-5
G = C // P
TILES = T // P
HG = P // HEAD
J4 = 4
SLOTS = HEAD // 2
LORA = 32
DECAY = 64
KINDS = ("w", "k", "v", "r", "g")
VECS = ("ln1_w", "ln1_b", "ln2_w", "ln2_b", "maa_x", "maa_w", "maa_k", "maa_v", "maa_r", "maa_g",
        "time_decay", "faaaa", "gn_w", "gn_b", "fmaa_k", "fmaa_r")
BIG = ("Wv", "Wk", "Wr", "Wg", "Wo", "fWr", "fWk", "fWv")
SMALL = ("vecs", "lora1", "lora2", "dec1", "second", "ident", "sel_v", "sel_r", "ones",
         "avg", "center", "states", "s0")
MIX_ORDER = ("w", "v", "k", "r", "g")
MULS = len(KINDS) * G
STACK = 3 * J4 * 16
ACT_JOBS = 5 * G + 2 * G + 2 + 2 + TILES + G
DVE_JOBS = MULS + 2 * TILES
PROJECTIONS = {
    0: [(0, 1, "v")], 1: [(0, 1, "k")], 2: [(0, 1, "w")], 3: [(0, 1, "r")], 7: [(0, 0, "g"), (0, 1, "g")],
    8: [(0, 2, "v")], 9: [(0, 2, "k")], 10: [(0, 2, "w"), (0, 2, "r"), (0, 2, "g")],
    16: [(0, 3, "v")], 18: [(0, 3, "r")], 19: [(0, 3, "k")], 20: [(0, 3, "w")],
    25: [(1, 0, "v")], 26: [(1, 0, "k")], 27: [(0, 3, "g"), (1, 0, "w")], 29: [(1, 0, "r")],
}
MIX_AT = {4: "g", 22: "w", 23: "v", 24: "k", 25: "r"}
OUT_AT = {5: (0, 1), 6: (2, 3)}
RECEPTANCE_AT = {11: (0, 1), 12: (2, 3)}
KEY_AT = {13: (0, 1), 14: (2, 3)}
VALUE_AT = {15: (0, 1), 16: (2,), 17: (3,)}
TOTAL_AT = {16: (0, 1), 17: (2, 3)}
LN2_NORM, LN2_TRANSPOSE, KEY_MIX, RECEPTANCE_MIX = 7, 8, 9, 10
LN1_STATS, LN1_NORM, LN1_TRANSPOSE, LOW_RANK_IN, LOW_RANK, DECAY_AT = 16, 17, 18, 19, 21, 24
STATE_BUF = [i % 3 for i in range(SLOTS)]
STATE_AGO = [2, 2, 5] + [3] * (SLOTS - 3)


def projections(b, slot, more):
    return [(b + ahead, g, kind) for ahead, g, kind in PROJECTIONS.get(slot, ()) if more or not ahead]


class Banks:

    def __init__(self, banks, jobs_per_row):
        self.banks, self.jobs, self.n, self.loop = banks, jobs_per_row, 0, 0
        self.read = [None, None]

    def take(self, read_sem=None, value=None, per_row=None):
        at = self.n % 2
        self.n += 1
        free, self.read[at] = self.read[at], (read_sem, value, per_row)
        return self.banks[at], self.loop + self.n, free

    def enter(self, b):
        self.first, self.loop, self.kept = self.n, (b - 1) * self.jobs, list(self.read)
        if self.read[0]:
            self.read = [(sem, value + (b - 1) * per, per) if per is not None else None for sem, value, per in self.read]

    def leave(self):
        assert self.n - self.first == self.jobs and self.jobs % 2 == 0
        rows = BATCH - 2
        self.n, self.loop = self.first + rows * self.jobs, 0
        if self.kept[0] and self.kept[0][2] is not None:
            assert all(a[0] is k[0] for a, k in zip(self.read, self.kept))
            self.read = [(sem, value + rows * per, per) for sem, value, per in self.kept]


def wait(eng, sem, value):
    if isinstance(value, int) and value <= 0:
        return
    eng.wait_ge(sem, value)


def rows_done(b, ahead):
    return min(b + ahead + 1, BATCH) if isinstance(b, int) else b + ahead + 1


def build(nc, dram, out):
    with ExitStack() as ctx:
        def sb(name, shape, dt=F32):
            return ctx.enter_context(nc.sbuf_tensor(name, shape, dt))

        def psum(name):
            return ctx.enter_context(nc.psum_tensor(name, [P, T], F32))

        def sem(name):
            return ctx.enter_context(nc.semaphore(name))

        W = {n: sb(f"W_{n}", [P, G, C]) for n in BIG}
        small = {n: sb(f"c_{n}", dram[n].shape, dram[n].dtype) for n in SMALL}
        vecs = small["vecs"]
        eps, half = sb("eps", [P, 1]), sb("half", [P, 1])
        wait_carrier = sb("wait_carrier", [P, 1])
        half_gn = sb("half_gn", [P, 2, G])

        def vec(name, c):
            return vecs[:, VECS.index(name), c:c + 1]

        bufA = sb("bufA", [P, TILES, C])
        bufB = sb("bufB", [P, G, T + 1])
        bufD = sb("bufD", [P, G, T])
        x1 = sb("x1", [P, TILES, C])
        mixed = {k: sb(f"mixed_{k}", [P, G, T]) for k in "kvrg"}
        mixed["w"] = bufA
        xxx = bufA
        t4 = sb("t4", [P, T])
        tanhs = sb("tanhs", [DECAY + LORA, T])
        td, tg = tanhs[0:DECAY, :], tanhs[DECAY:DECAY + LORA, :]
        stats, mv, sd = ({n: sb(f"{name}{n}", shape) for n in (1, 2)} for name, shape in
                         (("stats", [P, TILES, 6]), ("mv", [P, TILES, 2]), ("sd", [P, TILES])))

        pk, pr, pv, pw = (sb(n, [P, 2, T]) for n in ("pk", "pr", "pv", "pw"))
        gate = sb("gate", [P, G, T])
        v_hi, v_mid, v_lo = (sb(n, [P, T], BF16) for n in ("v_hi", "v_mid", "v_lo"))
        v_stack = sb("v_stack", [3 * 32, 2, J4, T], BF16)

        state = sb("state", [P, 3, 2, T + 1])
        diag = sb("diag", [P, T])
        fin_y = sb("fin_y", [P, T])
        fin_s = sb("fin_s", [P, T])
        yg = sb("yg", [P, G, T])

        ps_bc = [psum("ps_bc0"), psum("ps_bc1")]
        ps_y, ps_f = psum("ps_y"), psum("ps_f")
        ps_a = [psum("ps_a0"), psum("ps_a1")]
        ps_d = [psum("ps_d0"), psum("ps_d1")]

        big_in = {n: sem(f"{n}_in") for n in BIG}
        small_in, x_in, res_in, out_stored = sem("small_in"), sem("x_in"), sem("res_in"), sem("out_stored")
        stack_in = [sem("stack_in0"), sem("stack_in1")]
        consts_set = sem("consts_set")
        a_full, d_full = sem("a_full"), sem("d_full")
        bc_full, kv_set, s0_set, scan_set, rs_set, red_done = map(
            sem, ("bc_full", "kv_set", "s0_set", "scan_set", "rs_set", "red_done"))
        k_set, r_set, v_set, e_set, w_set, th_set, gate_set = map(
            sem, ("k_set", "r_set", "v_set", "e_set", "w_set", "th_set", "gate_set"))
        vhi_set, vrest_set, vmid_set, vlo_set = map(sem, ("vhi_set", "vrest_set", "vmid_set", "vlo_set"))
        diag_set, diag_full, dv_set, y_set, cen_full, yc_set, sq_set, var_full = map(
            sem, ("diag_set", "diag_full", "dv_set", "y_set", "cen_full", "yc_set", "sq_set", "var_full"))
        gsd_set, grs_set, yn_set, z_set, yg_set = map(sem, ("gsd_set", "grs_set", "yn_set", "z_set", "yg_set"))
        ln_stats, ln_aggr, ln_sd, ln_rs, ln_norm, ln_out, ln_edge = (
            {n: sem(f"ln{n}_{name}") for n in (1, 2)}
            for name in ("stats", "aggr", "sd", "rs", "norm", "out", "edge"))
        sx_set, xxx_set, t_set, mul_set, mix_set, td_set = map(
            sem, ("sx_set", "xxx_set", "t_set", "mul_set", "mix_set", "td_set"))
        x1_set, sxc_set, xk_set, xr_set, rth_set, rr_set, relu_set, kk_set, rk_set, sum_set = map(
            sem, ("x1_set", "sxc_set", "xk_set", "xr_set", "rth_set", "rr_set", "relu_set", "kk_set", "rk_set",
                  "sum_set"))

        gate_bank = {}
        x_rows = dram["x"].rearrange("b (n p) c -> b p n c", p=P)
        out_rows = out.rearrange("b (n p) c -> b p n c", p=P)

        def stack_loaded(b, g):
            return STACK * (2 * b + g // 2 + 1)

        block = ctx.enter_context(nc.Block())

        @block.sync
        def _(sp):
            def load_x(b):
                if isinstance(b, int) and b < 2:
                    wait(sp, td_set, 2 * b)
                else:
                    wait(sp, relu_set, G * (b - 1))
                sp.dma_start(bufA[:, :, :], x_rows[b]).then_inc(x_in, 16)

            def load_residual(b):
                wait(sp, out_stored, 16 * TILES * b)
                sp.dma_start(x1[:, :, :], x_rows[b]).then_inc(res_in, 16)

            def stack(b, g):
                s = G * b + g
                for part, (src, ready) in enumerate(((v_hi, vhi_set), (v_mid, vmid_set), (v_lo, vlo_set))):
                    wait(sp, ready, s + 1)
                    for q in range(J4):
                        sp.dma_start(v_stack[32 * part:32 * part + 32, g % 2, q, :],
                                     src[32 * q:32 * q + 32, :]).then_inc(stack_in[g % 2], 16)

            def store(b):
                for n in range(TILES):
                    wait(sp, sum_set, TILES * b + n + 1)
                    sp.dma_start(out_rows[b, :, n, :], x1[:, n, :]).then_inc(out_stored, 16)

            def row(b, prev, more):
                stack(b, 1)
                stack(b, 2)
                if more:
                    load_x(b + 1)
                stack(b, 3)
                if prev:
                    store(b - 1)
                load_residual(b)
                if more:
                    stack(b + 1, 0)

            load_x(0)
            for n in SMALL:
                sp.dma_start(small[n][:], dram[n]).then_inc(small_in, 16)
            for n in BIG:
                sp.dma_start(W[n][:, :, :], dram[n]).then_inc(big_in[n], 16)
            stack(0, 0)
            row(0, False, True)
            with sp.Fori(1, BATCH - 1) as b:
                row(b, True, True)
            row(BATCH - 1, True, False)
            store(BATCH - 1)
            sp.wait_ge(out_stored, 16 * TILES * BATCH)

        @block.tensor
        def _(pe):
            a_banks, d_banks = Banks(ps_a, ACT_JOBS), Banks(ps_d, DVE_JOBS)

            def bank_of(banks, read_sem, value, per_row):
                dst, _, free = banks.take(read_sem, value, per_row)
                if free:
                    wait(pe, free[0], free[1])
                return dst

            def product(dst, lhs, rhs):
                for c in range(G):
                    last = nc.tensor.matmul(dst, lhs(c), rhs(c), start=(c == 0), stop=(c == G - 1))
                return last

            def transposes(n, b):
                pe.wait_ge(ln_norm[n], TILES * (b + 1))
                for c in range(G):
                    dst = bank_of(a_banks, ln_out[n], G * b + c + 1, G)
                    for t in range(TILES):
                        last = nc.tensor.transpose(dst[:, P * t:P * t + P], bufA[:, t, P * c:P * c + P],
                                                   small["ident"][:])
                    last.then_inc(a_full, 1)

            def low_rank(b):
                pe.wait_ge(xxx_set, G * (b + 1))
                dst = bank_of(a_banks, t_set, 2 * b + 1, 2)
                product(dst[:, :], lambda c: small["lora1"][:, c, 0:P], lambda c: xxx[:, c, :]).then_inc(a_full, 1)
                dst = bank_of(a_banks, t_set, 2 * b + 2, 2)
                product(dst[DECAY:DECAY + LORA, :], lambda c: small["lora1"][:, c, P:P + LORA],
                        lambda c: xxx[:, c, :]).then_inc(a_full, 1)

            def mixes(b, kind, chunks):
                f = KINDS.index(kind)
                if chunks[0] == 0:
                    pe.wait_ge(t_set, 2 * (b + 1))
                for c in chunks:
                    dst = bank_of(d_banks, mul_set, MULS * b + G * MIX_ORDER.index(kind) + c + 1, MULS)
                    if kind == "g":
                        lhs, rhs = small["second"][DECAY:DECAY + LORA, P * c:P * c + P], tg
                    else:
                        lhs, rhs = small["lora2"][LORA * f:LORA * f + LORA, P * c:P * c + P], t4[LORA * f:LORA * f + LORA, :]
                    nc.tensor.matmul(dst[:, :], lhs, rhs, start=True, stop=True).then_inc(d_full, 1)

            def decay(b):
                pe.wait_ge(mix_set, MULS * b + G)
                for h in range(2):
                    dst = bank_of(a_banks, td_set, 2 * b + h + 1, 2)
                    product(dst[0:DECAY, 0:T // 2], lambda c: small["dec1"][:, c, :],
                            lambda c: bufA[:, c, T // 2 * h:T // 2 * (h + 1)]).then_inc(a_full, 1)

            def project(b, g, kind):
                s = G * b + g
                cols = slice(P * g, P * g + P)
                read_sem = {"v": vhi_set, "k": k_set, "w": e_set, "r": r_set, "g": gate_set}[kind]
                dst = bank_of(a_banks, read_sem, s + 1, G)
                if kind == "g":
                    assert gate_bank.setdefault(g, dst) is dst
                if kind == "w":
                    pe.wait_ge(td_set, 2 * (b + 1))
                    last = nc.tensor.matmul(dst[:, :], small["second"][0:DECAY, cols], td, start=True, stop=True)
                else:
                    pe.wait_ge(mix_set, MULS * b + G * (MIX_ORDER.index(kind) + 1))
                    w = W["W" + kind]
                    last = product(dst[:, :], lambda c: w[:, c, cols], lambda c: mixed[kind][:, c, :])
                last.then_inc(a_full, 1)

            def broadcast(b, g, j):
                wait(pe, kv_set, (G * b + g) * HEAD + j - 1)
                nc.tensor.matmul(ps_bc[j % 2][:, :], small["sel_v"][:, j % J4, :],
                                 v_stack[:, g % 2, j // J4, :], start=True, stop=True).then_inc(bc_full, 1)

            def reduce(b, g, i):
                s = G * b + g
                pe.wait_ge(rs_set, SLOTS * s + i + 1)
                if i == 0:
                    wait(pe, y_set, s)
                for e in range(2):
                    j = 2 * i + e
                    q = j // J4
                    last = nc.tensor.matmul(ps_y[32 * q:32 * q + 32, :], small["sel_r"][:, j % J4, :],
                                            state[:, STATE_BUF[i], e, 0:T], start=(j % J4 == 0), stop=(j % J4 == J4 - 1))
                last.then_inc(red_done, 1)

            def diagonal(s):
                pe.wait_ge(diag_set, s + 1)
                wait(pe, gsd_set, s)
                nc.tensor.matmul(ps_f[:, :], small["ones"][:], diag[:, :], start=True, stop=True).then_inc(diag_full, 1)

            def centre(s):
                pe.wait_ge(y_set, s + 1)
                nc.tensor.matmul(ps_f[:, :], small["center"][:], fin_y[:, :], start=True, stop=True).then_inc(cen_full, 1)

            def variance(s):
                pe.wait_ge(sq_set, s + 1)
                nc.tensor.matmul(ps_f[:, :], small["avg"][:], fin_s[:, :], start=True, stop=True).then_inc(var_full, 1)

            def out_proj(b, t):
                dst = bank_of(d_banks, x1_set, TILES * b + t + 1, TILES)
                pe.wait_ge(yg_set, G * (b + 1))
                product(dst[:, :], lambda c: yg[:, c, P * t:P * t + P], lambda c: W["Wo"][:, c, :]).then_inc(d_full, 1)

            def receptance(b, t):
                dst = bank_of(a_banks, rth_set, TILES * b + t + 1, TILES)
                pe.wait_ge(xr_set, G * (b + 1))
                product(dst[:, :], lambda c: bufD[:, c, P * t:P * t + P], lambda c: W["fWr"][:, c, :]).then_inc(a_full, 1)

            def key(b, f):
                dst = bank_of(a_banks, relu_set, G * b + f + 1, G)
                pe.wait_ge(xk_set, G * (b + 1))
                product(dst[:, :], lambda c: W["fWk"][:, c, P * f:P * f + P], lambda c: bufA[:, c, :]).then_inc(a_full, 1)

            def value(b, t):
                dst = bank_of(d_banks, rk_set, TILES * b + t + 1, TILES)
                pe.wait_ge(kk_set, G * (b + 1))
                product(dst[:, :], lambda c: bufD[:, c, P * t:P * t + P], lambda c: W["fWv"][:, c, :]).then_inc(d_full, 1)

            def row(b, prev, more):
                for slot in range(G * SLOTS):
                    g, i = divmod(slot, SLOTS)
                    s = G * b + g
                    finish = g > 0 or prev
                    if i == 0:
                        pe.wait_ge(stack_in[g % 2], stack_loaded(b, g))
                    broadcast(b, g, 2 * i)
                    broadcast(b, g, 2 * i + 1)
                    if finish and i == 2:
                        variance(s - 1)
                    kind = MIX_AT.get(slot)
                    mix = kind and (more or kind == "g")
                    if mix:
                        mixes(b + (kind != "g"), kind, (0, 1))
                    if prev:
                        for t in OUT_AT.get(slot, ()):
                            out_proj(b - 1, t)
                        for t in RECEPTANCE_AT.get(slot, ()):
                            receptance(b - 1, t)
                        for f in KEY_AT.get(slot, ()):
                            key(b - 1, f)
                        for t in VALUE_AT.get(slot, ()):
                            value(b - 1, t)
                    if more and slot == LOW_RANK:
                        low_rank(b + 1)
                    if more and slot == DECAY_AT:
                        decay(b + 1)
                    for at in projections(b, slot, more):
                        project(*at)
                    if finish and i == 1:
                        centre(s - 1)
                    if i == 6:
                        diagonal(s)
                    if prev and slot == LN2_TRANSPOSE:
                        transposes(2, b - 1)
                    if more and slot == LN1_TRANSPOSE:
                        transposes(1, b + 1)
                    if mix:
                        mixes(b + (kind != "g"), kind, (2, 3))
                    if i > 0:
                        reduce(b, g, i - 1)
                    elif g > 0:
                        reduce(b, g - 1, SLOTS - 1)
                    elif prev:
                        reduce(b - 1, G - 1, SLOTS - 1)

            pe.wait_ge(small_in, 16 * len(SMALL))
            transposes(1, 0)
            low_rank(0)
            mixes(0, "w", range(G))
            mixes(0, "v", range(G))
            decay(0)
            mixes(0, "k", range(G))
            pe.wait_ge(big_in["Wv"], 16)
            project(0, 0, "v")
            mixes(0, "r", range(G))
            project(0, 0, "w")
            pe.wait_ge(big_in["Wk"], 16)
            project(0, 0, "k")
            pe.wait_ge(big_in["Wr"], 16)
            project(0, 0, "r")
            pe.wait_ge(big_in["Wg"], 16)
            row(0, False, True)
            for n in ("Wo", "fWr", "fWk", "fWv"):
                pe.wait_ge(big_in[n], 16)
            with pe.Fori(1, BATCH - 1) as b:
                a_banks.enter(b)
                d_banks.enter(b)
                row(b, True, True)
            a_banks.leave()
            d_banks.leave()
            last = BATCH - 1
            row(last, True, False)
            reduce(last, G - 1, SLOTS - 1)
            centre(G * BATCH - 1)
            variance(G * BATCH - 1)
            for t in range(TILES):
                out_proj(last, t)
            transposes(2, last)
            for t in range(TILES):
                receptance(last, t)
            for f in range(G):
                key(last, f)
            for t in range(TILES):
                value(last, t)

        @block.scalar
        def _(act):
            banks = Banks(ps_a, ACT_JOBS)

            def job():
                src, number, _ = banks.take()
                act.wait_ge(a_full, number)
                return src

            def norm_sd(n, b):
                act.wait_ge(ln_aggr[n], TILES * (b + 1))
                nc.scalar.activation(sd[n][:, :], mv[n][:, :, 1], ACT.Sqrt, bias=eps[:, :]).then_inc(ln_sd[n], 1)

            def norm_out(n, b):
                if n == 1:
                    wait(act, mix_set, MULS * b)
                    wait(act, sum_set, TILES * (b - 1))
                else:
                    act.wait_ge(mix_set, MULS * rows_done(b, 1))
                for c in range(G):
                    src = job()
                    nc.scalar.activation(bufB[:, c, 1:T + 1], src[:, :], ACT.Identity, bias=vec(f"ln{n}_b", c),
                                         scale=vec(f"ln{n}_w", c)).then_inc(ln_out[n], 1)

            def low_rank(b):
                wait(act, mul_set, MULS * b)
                nc.scalar.activation(t4[:, :], job()[:, :], ACT.Tanh).then_inc(t_set, 1)
                nc.scalar.activation(tg, job()[DECAY:DECAY + LORA, :], ACT.Tanh).then_inc(t_set, 1)

            def decay(b):
                wait(act, e_set, G * b)
                for h in range(2):
                    nc.scalar.activation(tanhs[0:DECAY, T // 2 * h:T // 2 * (h + 1)], job()[0:DECAY, 0:T // 2],
                                         ACT.Tanh).then_inc(td_set, 1)

            def project(b, g, kind):
                s, par = G * b + g, g % 2
                src = job()
                if kind == "v":
                    wait(act, dv_set, s - 1)
                    nc.scalar.activation(pv[:, par, :], src[:, :], ACT.Copy).then_inc(v_set, 1)
                    wait(act, bc_full, HEAD * (s - 1))
                    if isinstance(s, int) and s == 0:
                        pass
                    elif g > 0:
                        act.wait_ge(stack_in[(g - 1) % 2], stack_loaded(b, g - 1))
                    else:
                        act.wait_ge(stack_in[1], stack_loaded(b - 1, G - 1))
                    nc.scalar.activation(v_hi[:, :], src[:, :], ACT.Copy).then_inc(vhi_set, 1)
                elif kind == "k":
                    wait(act, kv_set, HEAD * (s - 1))
                    wait(act, diag_set, s - 1)
                    nc.scalar.activation(pk[:, par, :], src[:, :], ACT.Copy).then_inc(k_set, 1)
                elif kind == "r":
                    wait(act, rs_set, SLOTS * (s - 1))
                    wait(act, diag_set, s - 1)
                    act.wait_ge(vlo_set, s + 1)
                    nc.scalar.activation(pr[:, par, :], src[:, :], ACT.Copy).then_inc(r_set, 1)
                elif kind == "w":
                    wait(act, scan_set, HEAD * (s - 1))
                    nc.scalar.activation(pw[:, par, :], src[:, :], ACT.Exp, bias=vec("time_decay", g)).then_inc(e_set, 1)
                    act.wait_ge(e_set, s + 1)
                    nc.scalar.activation(pw[:, par, :], pw[:, par, :], ACT.Exp, scale=-1.0).then_inc(w_set, 1)
                else:
                    wait(act, yg_set, s + 1 - G)
                    nc.scalar.activation(gate[:, g, :], src[:, :], ACT.Tanh, scale=0.5).then_inc(th_set, 1)

            def v_middle(s, g):
                act.wait_ge(vrest_set, s + 1)
                nc.scalar.activation(v_mid[:, :], pr[:, g % 2, :], ACT.Copy).then_inc(vmid_set, 1)

            def centred(s):
                act.wait_ge(cen_full, s + 1)
                nc.scalar.activation(fin_y[:, :], ps_f[:, :], ACT.Copy).then_inc(yc_set, 1)
                wait(act, yn_set, s)
                nc.scalar.activation(fin_s[:, :], ps_f[:, :], ACT.Square).then_inc(sq_set, 1)

            def group_sd(s):
                act.wait_ge(var_full, s + 1)
                nc.scalar.activation(fin_s[:, :], ps_f[:, :], ACT.Sqrt, bias=eps[:, :]).then_inc(gsd_set, 1)

            def group_affine(s, g):
                act.wait_ge(yn_set, s + 1)
                nc.scalar.activation(fin_y[:, :], fin_y[:, :], ACT.Identity, bias=half_gn[:, 1, g:g + 1],
                                     scale=half_gn[:, 0, g:g + 1]).then_inc(z_set, 1)

            def receptance(b, t):
                nc.scalar.activation(bufB[:, t, 0:T], job()[:, :], ACT.Tanh, scale=0.5).then_inc(rth_set, 1)
                act.wait_ge(rth_set, TILES * b + t + 1)
                nc.scalar.activation(bufB[:, t, 0:T], bufB[:, t, 0:T], ACT.Identity, bias=half[:, :],
                                     scale=0.5).then_inc(rr_set, 1)

            def key(b, f):
                if f == 0:
                    act.wait_ge(rth_set, TILES * (b + 1))
                nc.scalar.activation(bufD[:, f, :], job()[:, :], ACT.Relu).then_inc(relu_set, 1)
                act.wait_ge(relu_set, G * b + f + 1)
                nc.scalar.activation(bufD[:, f, :], bufD[:, f, :], ACT.Square).then_inc(kk_set, 1)

            def row(b, prev, more):
                for slot in range(G * SLOTS):
                    g, i = divmod(slot, SLOTS)
                    s = G * b + g
                    finish = g > 0 or prev
                    if finish and i == 4:
                        group_affine(s - 1, (g - 1) % G)
                    if finish and i == 2:
                        group_sd(s - 1)
                    if prev:
                        if slot == LN2_NORM - 1:
                            norm_sd(2, b - 1)
                        for t in RECEPTANCE_AT.get(slot, ()):
                            receptance(b - 1, t)
                        for f in KEY_AT.get(slot, ()):
                            key(b - 1, f)
                    if more and slot == LN1_NORM - 1:
                        norm_sd(1, b + 1)
                    if more and slot == LOW_RANK:
                        low_rank(b + 1)
                    if more and slot == DECAY_AT:
                        decay(b + 1)
                    for row_, group, kind in projections(b, slot - 1, more):
                        if kind == "v":
                            v_middle(G * row_ + group, group)
                    for at in projections(b, slot, more):
                        project(*at)
                    if finish and i == 1:
                        centred(s - 1)
                    if prev and slot == LN2_TRANSPOSE:
                        norm_out(2, b - 1)
                    if more and slot == LN1_TRANSPOSE:
                        norm_out(1, b + 1)

            act.wait_ge(small_in, 16 * len(SMALL))
            act.wait_ge(consts_set, 3)
            norm_sd(1, 0)
            norm_out(1, 0)
            low_rank(0)
            decay(0)
            project(0, 0, "v")
            v_middle(0, 0)
            for kind in "wkr":
                project(0, 0, kind)
            row(0, False, True)
            with act.Fori(1, BATCH - 1) as b:
                banks.enter(b)
                row(b, True, True)
            banks.leave()
            last = BATCH - 1
            row(last, True, False)
            centred(G * BATCH - 1)
            group_sd(G * BATCH - 1)
            group_affine(G * BATCH - 1, G - 1)
            norm_sd(2, last)
            norm_out(2, last)
            for t in range(TILES):
                receptance(last, t)
            for f in range(G):
                key(last, f)

        @block.vector
        def _(dve):
            banks = Banks(ps_d, DVE_JOBS)

            def job():
                src, number, _ = banks.take()
                dve.wait_ge(d_full, number)
                return src

            def pair(b, g, i):
                s, par, two = G * b + g, g % 2, state[:, STATE_BUF[i]]
                if i == 0:
                    dve.wait_ge(k_set, s + 1)
                wait(dve, red_done, SLOTS * s + i + 1 - STATE_AGO[i])
                nc.vector.tensor_copy(two[:, :, 0], small["s0"][:, b, g, 2 * i:2 * i + 2]).then_inc(s0_set, 1)
                for e in range(2):
                    dve.wait_ge(bc_full, HEAD * s + 2 * i + e + 1)
                    nc.vector.tensor_tensor(two[:, e, 1:T + 1], ps_bc[e][:, :], pk[:, par, :], ALU.mult)\
                        .then_inc(kv_set, 1)
                if i == 0:
                    dve.wait_ge(w_set, s + 1)
                dve.wait_ge(s0_set, SLOTS * s + i + 1)
                for e in range(2):
                    dve.wait_ge(kv_set, HEAD * s + 2 * i + e + 1)
                    nc.vector.tensor_tensor_scan(two[:, e, 1:T + 1], pw[:, par, :], two[:, e, 1:T + 1],
                                                 two[:, e, 0:1], ALU.mult, ALU.add).then_inc(scan_set, 1)

            def diagonal(b, g):
                s, par = G * b + g, g % 2
                dve.wait_ge(r_set, s + 1)
                wait(dve, y_set, s)
                nc.vector.scalar_tensor_tensor(diag[:, :], pr[:, par, :], vec("faaaa", g), pk[:, par, :],
                                               ALU.mult, ALU.mult).then_inc(diag_set, 1)

            def diagonal_v(b, g):
                s = G * b + g
                dve.wait_ge(diag_full, s + 1)
                dve.wait_ge(v_set, s + 1)
                nc.vector.tensor_tensor(diag[:, :], ps_f[:, :], pv[:, g % 2, :], ALU.mult).then_inc(dv_set, 1)

            def sum_y(s):
                dve.wait_ge(red_done, SLOTS * (s + 1))
                dve.wait_ge(dv_set, s + 1)
                wait(dve, yg_set, s)
                nc.vector.tensor_tensor(fin_y[:, :], ps_y[:, :], diag[:, :], ALU.add).then_inc(y_set, 1)

            def group_rs(s):
                dve.wait_ge(gsd_set, s + 1)
                nc.vector.reciprocal(fin_s[:, :], fin_s[:, :]).then_inc(grs_set, 1)

            def gate_silu(b, g):
                dve.wait_ge(th_set, G * b + g + 1)
                nc.vector.scalar_tensor_tensor(gate[:, g, :], gate[:, g, :], 1.0,
                                               gate_bank[g][:, :], ALU.add, ALU.mult).then_inc(gate_set, 1)

            def norm_stats(n, src, b, t):
                nc.vector.bn_stats(stats[n][:, t, :], src[:, t, :]).then_inc(ln_stats[n], 1)

            def norm_aggr(n, b):
                dve.wait_ge(ln_stats[n], TILES * (b + 1))
                nc.vector.memset(wait_carrier[:, :], 0.0)
                for t in range(TILES):
                    nc.vector.bn_aggr(mv[n][:, t, :], stats[n][:, t, :]).then_inc(ln_aggr[n], 1)

            def norm(n, src, b):
                dve.wait_ge(ln_sd[n], b + 1)
                nc.vector.reciprocal(sd[n][:, :], sd[n][:, :]).then_inc(ln_rs[n], 1)
                dve.wait_ge(ln_rs[n], b + 1)
                if n == 2:
                    dve.wait_ge(td_set, 2 * rows_done(b, 1))
                for t in range(TILES):
                    nc.vector.tensor_scalar(bufA[:, t, :], src[:, t, :], mv[n][:, t, 0:1], sd[n][:, t:t + 1],
                                            ALU.subtract, ALU.mult).then_inc(ln_norm[n], 1)

            def shift(n, b, done):
                dve.wait_ge(ln_edge[n], b + 1)
                if n == 1:
                    wait(dve, rk_set, TILES * (b - 1))
                    wait(dve, mul_set, MULS * b)
                else:
                    dve.wait_ge(mul_set, MULS * rows_done(b, 1))
                for c in range(G):
                    dve.wait_ge(ln_out[n], G * b + c + 1)
                    nc.vector.tensor_tensor(bufD[:, c, :], bufB[:, c, 0:T], bufB[:, c, 1:T + 1], ALU.subtract)\
                        .then_inc(done, 1)

            def low_rank_in(b):
                dve.wait_ge(ln_out[1], G * (b + 1))
                for c in range(G):
                    dve.wait_ge(sx_set, G * b + c + 1)
                    nc.vector.scalar_tensor_tensor(xxx[:, c, :], bufD[:, c, :], vec("maa_x", c), bufB[:, c, 1:T + 1],
                                                   ALU.mult, ALU.add).then_inc(xxx_set, 1)

            def mixes(b, kind):
                if kind == "w":
                    dve.wait_ge(t_set, 2 * (b + 1))
                else:
                    wait(dve, {"v": vhi_set, "k": k_set, "r": r_set, "g": gate_set}[kind], G * b)
                for c in range(G):
                    src = job()
                    nc.vector.scalar_tensor_tensor(mixed[kind][:, c, :], src[:, :], vec(f"maa_{kind}", c), bufD[:, c, :],
                                                   ALU.add, ALU.mult).then_inc(mul_set, 1)

            def residual(b, t):
                if t == 0:
                    dve.wait_ge(res_in, 16 * (b + 1))
                src = job()
                nc.vector.tensor_tensor(x1[:, t, :], src[:, :], x1[:, t, :], ALU.add).then_inc(x1_set, 1)
                dve.wait_ge(x1_set, TILES * b + t + 1)
                norm_stats(2, x1, b, t)

            def channel_mix(b, name, into, done):
                for c in range(G):
                    if name == "fmaa_k":
                        dve.wait_ge(sxc_set, G * b + c + 1)
                    nc.vector.scalar_tensor_tensor(into[:, c, :], bufD[:, c, :], vec(name, c), bufB[:, c, 1:T + 1],
                                                   ALU.mult, ALU.add).then_inc(done, 1)

            def key_mix(b):
                dve.wait_ge(ln_out[2], G * (b + 1))
                channel_mix(b, "fmaa_k", bufA, xk_set)

            def receptance_mix(b):
                dve.wait_ge(xk_set, G * (b + 1))
                channel_mix(b, "fmaa_r", bufD, xr_set)

            def value(b, t):
                dve.wait_ge(rr_set, TILES * b + t + 1)
                src = job()
                nc.vector.tensor_tensor(bufB[:, t, 0:T], src[:, :], bufB[:, t, 0:T], ALU.mult).then_inc(rk_set, 1)

            def row(b, prev, more):
                for slot in range(G * SLOTS):
                    g, i = divmod(slot, SLOTS)
                    s = G * b + g
                    finish = g > 0 or prev
                    if finish and i == 1:
                        sum_y(s - 1)
                    pair(b, g, i)
                    if finish and i == 2:
                        group_rs(s - 1)
                    if i == 5:
                        diagonal(b, g)
                    if i == 7:
                        diagonal_v(b, g)
                    for row_, group, kind in projections(b, slot, more):
                        if kind == "g":
                            gate_silu(row_, group)
                    kind = MIX_AT.get(slot)
                    if kind and (more or kind == "g"):
                        mixes(b + (kind != "g"), kind)
                    if prev:
                        for t in OUT_AT.get(slot, ()):
                            residual(b - 1, t)
                        if slot == LN2_NORM - 1:
                            norm_aggr(2, b - 1)
                        if slot == LN2_NORM:
                            norm(2, x1, b - 1)
                        if slot == KEY_MIX:
                            shift(2, b - 1, sxc_set)
                            key_mix(b - 1)
                        if slot == RECEPTANCE_MIX:
                            receptance_mix(b - 1)
                        for t in VALUE_AT.get(slot, ()):
                            value(b - 1, t)
                    if more and slot == LN1_STATS:
                        dve.wait_ge(x_in, 16 * (b + 2))
                        for t in range(TILES):
                            norm_stats(1, bufA, b + 1, t)
                        norm_aggr(1, b + 1)
                    if more and slot == LN1_NORM:
                        norm(1, bufA, b + 1)
                    if more and slot == LOW_RANK_IN:
                        shift(1, b + 1, sx_set)
                        low_rank_in(b + 1)

            nc.vector.memset(eps[:, :], EPS).then_inc(consts_set, 1)
            nc.vector.memset(half[:, :], 0.5).then_inc(consts_set, 1)
            dve.wait_ge(small_in, 16 * len(SMALL))
            n = VECS.index("gn_w")
            nc.vector.tensor_scalar(half_gn[:, :, :], vecs[:, n:n + 2, :], 0.5, None, ALU.mult).then_inc(consts_set, 1)
            dve.wait_ge(x_in, 16)
            for t in range(TILES):
                norm_stats(1, bufA, 0, t)
            norm_aggr(1, 0)
            norm(1, bufA, 0)
            shift(1, 0, sx_set)
            low_rank_in(0)
            for kind in MIX_ORDER[:-1]:
                mixes(0, kind)
            row(0, False, True)
            with dve.Fori(1, BATCH - 1) as b:
                banks.enter(b)
                row(b, True, True)
            banks.leave()
            last = BATCH - 1
            row(last, True, False)
            sum_y(G * BATCH - 1)
            group_rs(G * BATCH - 1)
            for t in range(TILES):
                residual(last, t)
            norm_aggr(2, last)
            norm(2, x1, last)
            shift(2, last, sxc_set)
            key_mix(last)
            receptance_mix(last)
            for t in range(TILES):
                value(last, t)

        @block.gpsimd
        def _(pool):
            def read_out(b, g, i):
                s = G * b + g
                if i == 0:
                    pool.wait_ge(r_set, s + 1)
                pool.wait_ge(scan_set, HEAD * s + 2 * i + 2)
                nc.gpsimd.tensor_tensor(state[:, STATE_BUF[i], :, 0:T], state[:, STATE_BUF[i], :, 0:T],
                                        pr[:, g % 2, :].unsqueeze(1).to_broadcast([P, 2, T]), ALU.mult)\
                    .then_inc(rs_set, 1)

            def v_less_first(s, g):
                wait(pool, rs_set, SLOTS * (s - 1))
                wait(pool, diag_set, s - 1)
                pool.wait_ge(vhi_set, s + 1)
                nc.gpsimd.tensor_tensor(pr[:, g % 2, :], pv[:, g % 2, :], v_hi[:, :], ALU.subtract).then_inc(vrest_set, 1)

            def v_third(s, g):
                pool.wait_ge(vmid_set, s + 1)
                nc.gpsimd.tensor_tensor(v_lo[:, :], pr[:, g % 2, :], v_mid[:, :], ALU.subtract).then_inc(vlo_set, 1)

            def normalise_y(s):
                pool.wait_ge(grs_set, s + 1)
                nc.gpsimd.tensor_tensor(fin_y[:, :], fin_y[:, :], fin_s[:, :], ALU.mult).then_inc(yn_set, 1)

            def gated_y(b, g):
                s = G * b + g
                pool.wait_ge(z_set, s + 1)
                pool.wait_ge(gate_set, s + 1)
                if g == 0:
                    wait(pool, x1_set, TILES * b)
                nc.gpsimd.tensor_tensor(yg[:, g, :], fin_y[:, :], gate[:, g, :], ALU.mult).then_inc(yg_set, 1)

            def edge(n, b):
                if n == 1:
                    wait(pool, mix_set, MULS * b)
                    wait(pool, sum_set, TILES * (b - 1))
                else:
                    pool.wait_ge(mix_set, MULS * rows_done(b, 1))
                nc.gpsimd.tensor_copy(bufB[:, :, 0], small["states"][:, b, n - 1, :]).then_inc(ln_edge[n], 1)

            def mixes(b, kind):
                for c in range(G):
                    pool.wait_ge(mul_set, MULS * b + G * MIX_ORDER.index(kind) + c + 1)
                    nc.gpsimd.tensor_tensor(mixed[kind][:, c, :], mixed[kind][:, c, :], bufB[:, c, 1:T + 1], ALU.add)\
                        .then_inc(mix_set, 1)

            def total(b, t):
                pool.wait_ge(rk_set, TILES * b + t + 1)
                nc.gpsimd.tensor_tensor(x1[:, t, :], x1[:, t, :], bufB[:, t, 0:T], ALU.add).then_inc(sum_set, 1)

            def row(b, prev, more):
                for slot in range(G * SLOTS):
                    g, i = divmod(slot, SLOTS)
                    s = G * b + g
                    finish = g > 0 or prev
                    read_out(b, g, i)
                    if finish and i == 3:
                        normalise_y(s - 1)
                    if finish and i == 4:
                        gated_y(*((b, g - 1) if g > 0 else (b - 1, G - 1)))
                    for row_, group, kind in projections(b, slot - 1, more):
                        if kind == "v":
                            v_third(G * row_ + group, group)
                    for row_, group, kind in projections(b, slot, more):
                        if kind == "v":
                            v_less_first(G * row_ + group, group)
                    kind = MIX_AT.get(slot)
                    if kind and (more or kind == "g"):
                        mixes(b + (kind != "g"), kind)
                    if prev and slot == LN2_TRANSPOSE:
                        edge(2, b - 1)
                    if prev:
                        for t in TOTAL_AT.get(slot, ()):
                            total(b - 1, t)
                    if more and slot == LN1_TRANSPOSE:
                        edge(1, b + 1)

            pool.wait_ge(small_in, 16 * len(SMALL))
            edge(1, 0)
            for kind in MIX_ORDER[:-1]:
                mixes(0, kind)
            v_less_first(0, 0)
            v_third(0, 0)
            row(0, False, True)
            with pool.Fori(1, BATCH - 1) as b:
                row(b, True, True)
            last = BATCH - 1
            row(last, True, False)
            normalise_y(G * BATCH - 1)
            gated_y(last, G - 1)
            edge(2, last)
            for t in range(TILES):
                total(last, t)


def kernel(**inputs):
    import ml_dtypes
    import concourse.bacc as bacc
    from concourse.bass_utils import run_bass_kernel_spmd

    a = {k.replace("L0_xattn_", ""): np.asarray(v) for k, v in inputs.items()}
    jh = np.arange(C).reshape(G, HG, HEAD).transpose(0, 2, 1).reshape(C)

    def chunks(w):
        return np.ascontiguousarray(w.reshape(-1, P, w.shape[1]).transpose(1, 0, 2))

    def channel_major(v):
        v = v.reshape(v.shape[:-1] + (G, P))
        return np.moveaxis(v, -1, 0)

    vectors = dict(a, faaaa=a["faaaa"].reshape(C), gn_w=a["gn_w"][jh], gn_b=a["gn_b"][jh])
    ctx_rows = a["ctx_2048"]
    eye, row, col = np.eye(P, dtype=np.float32), np.arange(P)[:, None], np.arange(P)[None, :]
    same_head = (row % HG == col % HG).astype(np.float32)
    arrays = {
        "x": a["x"],
        "vecs": np.stack([channel_major(vectors[n]) for n in VECS], axis=1),
        "lora1": chunks(a["maa_w1"]),
        "lora2": a["maa_w2"][:4].reshape(4 * LORA, C),
        "dec1": chunks(a["decay_w1"]),
        "second": np.concatenate([a["decay_w2"], a["maa_w2"][4]]),
        "ident": eye,
        "sel_v": np.stack([((np.arange(96)[:, None] % 32) == HG * jj + col // HEAD) for jj in range(J4)], axis=1)
        .astype(ml_dtypes.bfloat16),
        "sel_r": np.stack([(np.arange(32)[None, :] == HG * jj + row // HEAD) for jj in range(J4)], axis=1)
        .astype(np.float32),
        "ones": (row // HEAD == col % HG).astype(np.float32),
        "avg": same_head / HEAD,
        "center": eye - same_head / HEAD,
        "states": channel_major(ctx_rows[:, [1, 0]]),
        "s0": ctx_rows[:, 2:2 + HEAD].reshape(BATCH, G, P, HEAD).transpose(2, 0, 1, 3),
        "Wv": chunks(a["Wv"].T[:, jh]), "Wg": chunks(a["Wg"].T[:, jh]),
        "Wk": chunks(a["Wk"].T), "Wr": chunks(a["Wr"].T), "Wo": chunks(a["Wo"].T[jh]),
        "fWr": chunks(a["fWr"].T), "fWk": chunks(a["fWk"].T), "fWv": chunks(a["fWv"].T),
    }
    arrays = {k: np.ascontiguousarray(v) for k, v in arrays.items()}
    nc = bacc.Bacc("TRN2", target_bir_lowering=False, num_devices=1)
    dram = {n: nc.dram_tensor(f"in_{n}", v.shape, mybir.dt.from_np(v.dtype), kind="ExternalInput").ap()
            for n, v in arrays.items()}
    out = nc.dram_tensor("out_0", (BATCH, T, C), F32, kind="ExternalOutput").ap()
    build(nc, dram, out)
    r = run_bass_kernel_spmd(nc, [{f"in_{n}": v for n, v in arrays.items()}], core_ids=[0])
    return r.results[0]["out_0"]
```

```python
from contextlib import ExitStack

import numpy as np

import concourse.bass as bass
from concourse import mybir

F32 = mybir.dt.float32
F32R = mybir.dt.float32r
BF16 = mybir.dt.bfloat16
ALU = mybir.AluOpType
ACT = mybir.ActivationFunctionType

P = 128
BATCH, T, C = 8, 512, 512
HEAD = 16
EPS = 1e-5
G = C // P
TILES = T // P
HG = P // HEAD
J4 = 4
SLOTS = HEAD // 2
LORA = 32
DECAY = 64
KINDS = ("w", "k", "v", "r", "g")
VECS = ("ln1_w", "ln1_b", "ln2_w", "ln2_b", "maa_x", "maa_w", "maa_k", "maa_v", "maa_r", "maa_g",
        "time_decay", "faaaa", "gn_w", "gn_b", "fmaa_k", "fmaa_r")
BIG = ("Wv", "Wk", "Wr", "Wg", "Wo", "fWr", "fWk", "fWv")
SMALL = ("vecs", "lora1", "dec1", "second", "ident", "sel_v", "sel_r", "ones",
         "avg", "center", "states")
MIX_ORDER = ("v", "w", "k", "r", "g")
MULS = len(KINDS) * G
TANHS = 7 + TILES
STACK = 3 * J4 * 16
ACT_JOBS = 5 * G + 2 * G + 2 + 2 + TILES + G
DVE_JOBS = MULS + 2 * TILES
PROJECTIONS = {
    0: [(0, 1, "v")], 3: [(0, 1, "w")], 4: [(0, 1, "k")], 5: [(0, 1, "r")], 7: [(0, 0, "g"), (0, 1, "g")],
    8: [(0, 2, "v")], 9: [(0, 2, "k")], 10: [(0, 2, "w"), (0, 2, "r")], 12: [(0, 2, "g")], 16: [(0, 3, "v")],
    19: [(0, 3, "r")], 20: [(0, 3, "w"), (0, 3, "k")], 27: [(1, 0, "k")], 28: [(1, 0, "w"), (1, 0, "v")],
    29: [(1, 0, "r")], 31: [(0, 3, "g")],
}
MIX_AT = {2: (("g", 0),), 4: (("g", 1),), 23: (("v", 0), ("v", 1)), 24: (("w", 0), ("w", 1)),
          25: (("k", 0), ("k", 1)), 26: (("r", 0),), 27: (("r", 1),)}
OUT_AT = {6: (0, 1, 2, 3)}
RECEPTANCE_AT = {11: (0,), 12: (1,), 13: (2, 3)}
KEY_AT = {14: (0, 1, 2, 3)}
VALUE_AT = {15: (0,), 16: (1,), 17: (2, 3)}
TOTAL_AT = {14: (0,), 15: (1,), 17: (2, 3)}
LN2_NORM, LN2_TRANSPOSE, KEY_MIX, RECEPTANCE_MIX = 7, 8, 9, 10
LN1_STATS, LN1_NORM, LN1_TRANSPOSE, LOW_RANK_IN, LOW_RANK, TANH_REST, DECAY_SLOT = 16, 16, 18, 19, 21, 21, 26
FINISH = {"centre": 1, "variance": 2, "rs": 2, "spread": 3, "normalise": 3, "affine": 3, "gated": 3,
          "diagonal": 5, "head_sums": 6, "diagonal_v": 7}
REDUCE_FIRST = (8, 10, 13, 18, 20, 23)
STATE_BUF = [i % 3 for i in range(SLOTS)]
STATE_AGO = [2, 2, 5] + [3] * (SLOTS - 3)


def projections(b, slot, more):
    return [(b + ahead, g, kind) for ahead, g, kind in PROJECTIONS.get(slot, ()) if more or not ahead]


def halves(b, slot, more):
    return [(b + (kind != "g"), kind, (2 * half, 2 * half + 1)) for kind, half in MIX_AT.get(slot, ())
            if more or kind == "g"]


class Banks:

    def __init__(self, banks, jobs_per_row):
        self.banks, self.jobs, self.n, self.loop = banks, jobs_per_row, 0, 0
        self.read = [None, None]

    def take(self, read_sem=None, value=None, per_row=None):
        at = self.n % 2
        self.n += 1
        free, self.read[at] = self.read[at], (read_sem, value, per_row)
        return self.banks[at], self.loop + self.n, free

    def enter(self, b):
        self.first, self.loop, self.kept = self.n, (b - 1) * self.jobs, list(self.read)
        if self.read[0]:
            self.read = [(sem, value + (b - 1) * per, per) if per is not None else None for sem, value, per in self.read]

    def leave(self):
        assert self.n - self.first == self.jobs and self.jobs % 2 == 0
        rows = BATCH - 2
        self.n, self.loop = self.first + rows * self.jobs, 0
        if self.kept[0] and self.kept[0][2] is not None:
            assert all(a[0] is k[0] for a, k in zip(self.read, self.kept))
            self.read = [(sem, value + rows * per, per) for sem, value, per in self.kept]


def wait(eng, sem, value):
    if isinstance(value, int) and value <= 0:
        return
    eng.wait_ge(sem, value)


def rows_done(b, ahead):
    return min(b + ahead + 1, BATCH) if isinstance(b, int) else b + ahead + 1


def build(nc, dram, out):
    with ExitStack() as ctx:
        def sb(name, shape, dt=F32):
            return ctx.enter_context(nc.sbuf_tensor(name, shape, dt))

        def psum(name):
            return ctx.enter_context(nc.psum_tensor(name, [P, T], F32))

        def sem(name):
            return ctx.enter_context(nc.semaphore(name))

        W = {n: sb(f"W_{n}", [P, G, C]) for n in BIG}
        small = {n: sb(f"c_{n}", dram[n].shape, dram[n].dtype) for n in SMALL}
        vecs = small["vecs"]
        eps, half = sb("eps", [P, 1]), sb("half", [P, 1])
        wait_carrier, unread = sb("wait_carrier", [P, 1]), sb("unread", [P, 1])
        half_gn = sb("half_gn", [P, 2, G])

        def vec(name, c):
            return vecs[:, VECS.index(name), c:c + 1]

        bufA = sb("bufA", [P, TILES, C])
        bufB = sb("bufB", [P, G, T + 1])
        bufD = sb("bufD", [P, G, T])
        x_next = sb("x_next", [P, TILES, C])
        with nc.sbuf_tensor("t_stack", [P, G, T], F32R) as t_stack:
            pass
        x1 = sb("x1", [P, TILES, C])
        mixed = {k: sb(f"mixed_{k}", [P, G, T]) for k in "kvrg"}
        mixed["w"] = bufA
        xxx = bufA
        t_raw, t_hi = mixed["v"][:, 3, :], mixed["v"][:, 2, :]
        mix_w = sb("mix_w", [P, len(KINDS) - 1, C], F32R)
        tanhs = sb("tanhs", [DECAY + LORA, T])
        td, tg = slice(0, DECAY), slice(DECAY, DECAY + LORA)
        s0 = sb("s0", [P, G, HEAD])
        stats, mv, sd = ({n: sb(f"{name}{n}", shape) for n in (1, 2)} for name, shape in
                         (("stats", [P, TILES, 6]), ("mv", [P, TILES, 2]), ("sd", [P, TILES])))

        pk, pr, pv, pw = (sb(n, [P, 2, T]) for n in ("pk", "pr", "pv", "pw"))
        gate = sb("gate", [P, G, T])
        v_hi, v_mid, v_lo = (sb(n, [P, T], BF16) for n in ("v_hi", "v_mid", "v_lo"))
        v_stack = sb("v_stack", [3 * 32, 2, J4, T], BF16)

        state = sb("state", [P, 3, 2, T + 1])
        fin_y = sb("fin_y", [P, T])
        fin_s = sb("fin_s", [P, T])
        head_sd = sb("head_sd", [P, TILES, HG])
        diag = fin_s

        ps_bc = [psum("ps_bc0"), psum("ps_bc1")]
        ps_y, ps_f = psum("ps_y"), psum("ps_f")
        ps_a = [psum("ps_a0"), psum("ps_a1")]
        ps_d = [psum("ps_d0"), psum("ps_d1")]

        big_in = {n: sem(f"{n}_in") for n in BIG}
        small_in, res_in, s0_in, out_stored = map(sem, ("small_in", "res_in", "s0_in", "out_stored"))
        x_in = [sem(f"x_in{t}") for t in range(TILES)]
        stack_in = [sem("stack_in0"), sem("stack_in1")]
        consts_set = sem("consts_set")
        mix_w_in, w_hi_set, mix_w_set, lo_set, stack_set = map(
            sem, ("mix_w_in", "w_hi_set", "mix_w_set", "lo_set", "stack_set"))
        a_full, d_full = sem("a_full"), sem("d_full")
        bc_full, kv_set, s0_set, scan_set, rs_set, red_done = map(
            sem, ("bc_full", "kv_set", "s0_set", "scan_set", "rs_set", "red_done"))
        k_set, r_set, v_set, e_set, w_set, th_set, gate_set = map(
            sem, ("k_set", "r_set", "v_set", "e_set", "w_set", "th_set", "gate_set"))
        vhi_set, vrest_set, vmid_set, vlo_set = map(sem, ("vhi_set", "vrest_set", "vmid_set", "vlo_set"))
        diag_set, diag_full, dv_set, y_set, cen_full, yc_set, sq_set, var_full = map(
            sem, ("diag_set", "diag_full", "dv_set", "y_set", "cen_full", "yc_set", "sq_set", "var_full"))
        gsd_set, grs_set, rep_set, rs_full, yn_set, z_set, yg_set = map(
            sem, ("gsd_set", "grs_set", "rep_set", "rs_full", "yn_set", "z_set", "yg_set"))
        ln_stats, ln_aggr, ln_sd, ln_rs, ln_norm, ln_out, ln_edge = (
            {n: sem(f"ln{n}_{name}") for n in (1, 2)}
            for name in ("stats", "aggr", "sd", "rs", "norm", "out", "edge"))
        sx_set, xxx_set, t_set, mul_set, mix_set, td_set = map(
            sem, ("sx_set", "xxx_set", "t_set", "mul_set", "mix_set", "td_set"))
        x1_set, sxc_set, xk_set, xr_set, rth_set, rr_set, relu_set, kk_set, rk_set, sum_set = map(
            sem, ("x1_set", "sxc_set", "xk_set", "xr_set", "rth_set", "rr_set", "relu_set", "kk_set", "rk_set",
                  "sum_set"))

        gate_bank = {}
        x_rows = dram["x"].rearrange("b (n p) c -> b p n c", p=P)
        out_rows = out.rearrange("b (n p) c -> b p n c", p=P)

        def stack_loaded(b, g):
            return STACK * (2 * b + g // 2 + 1)

        block = ctx.enter_context(nc.Block())

        @block.sync
        def _(sp):
            def load_x(b):
                wait(sp, ln_out[1], G * b)
                for t in range(TILES):
                    sp.dma_start(x_next[:, t, :], x_rows[b, :, t, :]).then_inc(x_in[t], 16)

            def load_s0(b, g):
                wait(sp, s0_set, SLOTS * (G * b + g + 1 - G))
                sp.dma_start(s0[:, g, :], dram["s0"][:, b, g, :]).then_inc(s0_in, 16)

            def load_residual(b, more):
                wait(sp, out_stored, 16 * TILES * b)
                if more:
                    wait(sp, mul_set, MULS * (b + 1) + 4 * G)
                sp.dma_start(x1[:, :, :], x_rows[b]).then_inc(res_in, 16)

            def stack(b, g):
                s = G * b + g
                for part, (src, ready) in enumerate(((v_hi, vhi_set), (v_mid, vmid_set), (v_lo, vlo_set))):
                    wait(sp, ready, s + 1)
                    for q in range(J4):
                        sp.dma_start(v_stack[32 * part:32 * part + 32, g % 2, q, :],
                                     src[32 * q:32 * q + 32, :]).then_inc(stack_in[g % 2], 16)

            def store(b):
                for n in range(TILES):
                    wait(sp, sum_set, TILES * b + n + 1)
                    sp.dma_start(out_rows[b, :, n, :], x1[:, n, :]).then_inc(out_stored, 16)

            def row(b, prev, more):
                load_s0(b, G - 1)
                if more:
                    load_x(b + 1)
                stack(b, 1)
                if more:
                    load_s0(b + 1, 0)
                stack(b, 2)
                if more:
                    load_s0(b + 1, 1)
                stack(b, 3)
                if prev:
                    store(b - 1)
                if more:
                    load_s0(b + 1, 2)
                    stack(b + 1, 0)
                load_residual(b, more)

            load_x(0)
            for n in SMALL:
                sp.dma_start(small[n][:], dram[n]).then_inc(small_in, 16)
            sp.dma_start(x1[:, :, :], dram["lora2"]).then_inc(mix_w_in, 16)
            for g in range(G - 1):
                load_s0(0, g)
            for n in BIG:
                sp.dma_start(W[n][:, :, :], dram[n]).then_inc(big_in[n], 16)
            stack(0, 0)
            row(0, False, True)
            with sp.Fori(1, BATCH - 1) as b:
                row(b, True, True)
            row(BATCH - 1, True, False)
            store(BATCH - 1)
            sp.wait_ge(out_stored, 16 * TILES * BATCH)

        @block.tensor
        def _(pe):
            a_banks, d_banks = Banks(ps_a, ACT_JOBS), Banks(ps_d, DVE_JOBS)

            def bank_of(banks, read_sem, value, per_row):
                dst, _, free = banks.take(read_sem, value, per_row)
                if free:
                    wait(pe, free[0], free[1])
                return dst

            def product(dst, lhs, rhs):
                for c in range(G):
                    last = nc.tensor.matmul(dst, lhs(c), rhs(c), start=(c == 0), stop=(c == G - 1))
                return last

            def transposes(n, b):
                rows = {1: x_next, 2: bufA}[n]
                pe.wait_ge(ln_norm[n], TILES * (b + 1))
                for c in range(G):
                    dst = bank_of(a_banks, ln_out[n], G * b + c + 1, G)
                    for t in range(TILES):
                        last = nc.tensor.transpose(dst[:, P * t:P * t + P], rows[:, t, P * c:P * c + P],
                                                   small["ident"][:])
                    last.then_inc(a_full, 1)

            def low_rank(b):
                pe.wait_ge(xxx_set, G * (b + 1))
                dst = bank_of(a_banks, t_set, TANHS * b + 6, TANHS)
                product(dst[:, :], lambda c: small["lora1"][:, c, 0:P], lambda c: xxx[:, c, :]).then_inc(a_full, 1)
                dst = bank_of(a_banks, t_set, TANHS * (b + 1), TANHS)
                for c in range(G):
                    for n in range(TILES):
                        last = nc.tensor.matmul(dst[LORA * n:LORA * n + LORA, 0:P], small["lora1"][:, c, P:P + LORA],
                                                xxx[:, c, P * n:P * n + P], start=(c == 0), stop=(c == G - 1))
                last.then_inc(a_full, 1)

            def mixes(b, kind, chunks):
                f = KINDS.index(kind)
                if chunks[0] == 0 and kind == "g":
                    pe.wait_ge(t_set, TANHS * (b + 1))
                elif chunks[0] == 0:
                    pe.wait_ge(t_set, TANHS * b + 7)
                    pe.wait_ge(stack_set, b + 1)
                for c in chunks:
                    dst = bank_of(d_banks, mul_set, MULS * b + G * MIX_ORDER.index(kind) + c + 1, MULS)
                    if kind == "g":
                        lhs, rhs = small["second"][tg, P * c:P * c + P], tanhs[tg, :]
                    else:
                        lhs, rhs = mix_w[:, f, P * c:P * c + P], t_stack[:, f, :]
                    nc.tensor.matmul(dst[:, :], lhs, rhs, start=True, stop=True).then_inc(d_full, 1)

            def decay(b):
                pe.wait_ge(mix_set, MULS * b + G * (MIX_ORDER.index("w") + 1))
                dst = [bank_of(a_banks, td_set, 2 * b + h + 1, 2) for h in range(2)]
                for c in range(G):
                    for h in range(2):
                        last = nc.tensor.matmul(dst[h][DECAY * h:DECAY * h + DECAY, 0:T // 2], small["dec1"][:, c, :],
                                                mixed["w"][:, c, T // 2 * h:T // 2 * (h + 1)], start=(c == 0), stop=(c == G - 1))
                        if c == G - 1:
                            last.then_inc(a_full, 1)

            def project(b, g, kind):
                s = G * b + g
                cols = slice(P * g, P * g + P)
                read_sem = {"v": vhi_set, "k": k_set, "w": e_set, "r": r_set, "g": gate_set}[kind]
                dst = bank_of(a_banks, read_sem, s + 1, G)
                if kind == "g":
                    assert gate_bank.setdefault(g, dst) is dst
                if kind == "w":
                    pe.wait_ge(td_set, 2 * (b + 1))
                    last = nc.tensor.matmul(dst[:, :], small["second"][td, cols], tanhs[td, :], start=True, stop=True)
                else:
                    pe.wait_ge(mix_set, MULS * b + G * (MIX_ORDER.index(kind) + 1))
                    w = W["W" + kind]
                    last = product(dst[:, :], lambda c: w[:, c, cols], lambda c: mixed[kind][:, c, :])
                last.then_inc(a_full, 1)

            def broadcast(b, g, j):
                wait(pe, kv_set, (G * b + g) * HEAD + j - 1)
                nc.tensor.matmul(ps_bc[j % 2][:, :], small["sel_v"][:, j % J4, :],
                                 v_stack[:, g % 2, j // J4, :], start=True, stop=True).then_inc(bc_full, 1)

            def reduce(b, g, i):
                s = G * b + g
                pe.wait_ge(rs_set, SLOTS * s + i + 1)
                if i == 0:
                    wait(pe, y_set, s)
                for e in range(2):
                    j = 2 * i + e
                    q = j // J4
                    last = nc.tensor.matmul(ps_y[32 * q:32 * q + 32, :], small["sel_r"][:, j % J4, :],
                                            state[:, STATE_BUF[i], e, 0:T], start=(j % J4 == 0), stop=(j % J4 == J4 - 1))
                last.then_inc(red_done, 1)

            def reduce_last(b, g, i, prev):
                if i > 0:
                    reduce(b, g, i - 1)
                elif g > 0:
                    reduce(b, g - 1, SLOTS - 1)
                elif prev:
                    reduce(b - 1, G - 1, SLOTS - 1)

            def diagonal(s):
                pe.wait_ge(diag_set, s + 1)
                wait(pe, yn_set, s)
                nc.tensor.matmul(ps_f[:, :], small["ones"][:], diag[:, :], start=True, stop=True).then_inc(diag_full, 1)

            def centre(s):
                pe.wait_ge(y_set, s + 1)
                nc.tensor.matmul(ps_f[:, :], small["center"][:], fin_y[:, :], start=True, stop=True).then_inc(cen_full, 1)

            def variance(s):
                pe.wait_ge(sq_set, s + 1)
                for t in range(TILES):
                    last = nc.tensor.matmul(ps_f[:, HG * t:HG * t + HG], fin_s[:, P * t:P * t + P], small["avg"][:],
                                            start=True, stop=True)
                last.then_inc(var_full, 1)

            def spread(s):
                pe.wait_ge(rep_set, s + 1)
                for t in range(TILES):
                    last = nc.tensor.transpose(ps_f[:, P * t:P * t + P],
                                               fin_s[:, P * t:P * t + P], small["ident"][:])
                last.then_inc(rs_full, 1)

            def out_proj(b, t):
                dst = bank_of(d_banks, x1_set, TILES * b + t + 1, TILES)
                pe.wait_ge(yg_set, G * (b + 1))
                product(dst[:, :], lambda c: gate[:, c, P * t:P * t + P], lambda c: W["Wo"][:, c, :]).then_inc(d_full, 1)

            def receptance(b, t):
                dst = bank_of(a_banks, rth_set, TILES * b + t + 1, TILES)
                pe.wait_ge(xr_set, G * (b + 1))
                product(dst[:, :], lambda c: bufD[:, c, P * t:P * t + P], lambda c: W["fWr"][:, c, :]).then_inc(a_full, 1)

            def key(b, f):
                dst = bank_of(a_banks, relu_set, G * b + f + 1, G)
                pe.wait_ge(xk_set, G * (b + 1))
                product(dst[:, :], lambda c: W["fWk"][:, c, P * f:P * f + P], lambda c: bufA[:, c, :]).then_inc(a_full, 1)

            def value(b, t):
                dst = bank_of(d_banks, rk_set, TILES * b + t + 1, TILES)
                pe.wait_ge(kk_set, G * (b + 1))
                product(dst[:, :], lambda c: bufD[:, c, P * t:P * t + P], lambda c: W["fWv"][:, c, :]).then_inc(d_full, 1)

            def row(b, prev, more):
                for slot in range(G * SLOTS):
                    g, i = divmod(slot, SLOTS)
                    s = G * b + g
                    finish = g > 0 or prev
                    if i == 0:
                        pe.wait_ge(stack_in[g % 2], stack_loaded(b, g))
                    broadcast(b, g, 2 * i)
                    broadcast(b, g, 2 * i + 1)
                    if slot in REDUCE_FIRST:
                        reduce_last(b, g, i, prev)
                    if finish and i == FINISH["variance"]:
                        variance(s - 1)
                    if finish and i == FINISH["spread"]:
                        spread(s - 1)
                    for at in halves(b, slot, more)[:1]:
                        mixes(*at)
                    if prev:
                        for t in OUT_AT.get(slot, ()):
                            out_proj(b - 1, t)
                        for t in RECEPTANCE_AT.get(slot, ()):
                            receptance(b - 1, t)
                        for f in KEY_AT.get(slot, ()):
                            key(b - 1, f)
                        for t in VALUE_AT.get(slot, ()):
                            value(b - 1, t)
                    if more and slot == LOW_RANK:
                        low_rank(b + 1)
                    if more and slot == DECAY_SLOT:
                        decay(b + 1)
                    for at in projections(b, slot, more):
                        project(*at)
                    if finish and i == FINISH["centre"]:
                        centre(s - 1)
                    if i == FINISH["head_sums"]:
                        diagonal(s)
                    if prev and slot == LN2_TRANSPOSE:
                        transposes(2, b - 1)
                    if more and slot == LN1_TRANSPOSE:
                        transposes(1, b + 1)
                    for at in halves(b, slot, more)[1:]:
                        mixes(*at)
                    if slot not in REDUCE_FIRST:
                        reduce_last(b, g, i, prev)

            pe.wait_ge(small_in, 16 * len(SMALL))
            transposes(1, 0)
            low_rank(0)
            mixes(0, "v", range(G))
            mixes(0, "w", range(G))
            pe.wait_ge(big_in["Wv"], 16)
            project(0, 0, "v")
            mixes(0, "k", range(G))
            decay(0)
            mixes(0, "r", range(G))
            project(0, 0, "w")
            pe.wait_ge(big_in["Wk"], 16)
            project(0, 0, "k")
            pe.wait_ge(big_in["Wr"], 16)
            project(0, 0, "r")
            pe.wait_ge(big_in["Wg"], 16)
            row(0, False, True)
            for n in ("Wo", "fWr", "fWk", "fWv"):
                pe.wait_ge(big_in[n], 16)
            with pe.Fori(1, BATCH - 1) as b:
                a_banks.enter(b)
                d_banks.enter(b)
                row(b, True, True)
            a_banks.leave()
            d_banks.leave()
            last = BATCH - 1
            row(last, True, False)
            reduce(last, G - 1, SLOTS - 1)
            centre(G * BATCH - 1)
            variance(G * BATCH - 1)
            spread(G * BATCH - 1)
            for t in range(TILES):
                out_proj(last, t)
            transposes(2, last)
            for t in range(TILES):
                receptance(last, t)
            for f in range(G):
                key(last, f)
            for t in range(TILES):
                value(last, t)

        @block.scalar
        def _(act):
            banks = Banks(ps_a, ACT_JOBS)

            def job():
                src, number, _ = banks.take()
                act.wait_ge(a_full, number)
                return src

            def norm_sd(n, b):
                act.wait_ge(ln_aggr[n], TILES * (b + 1))
                nc.scalar.activation(sd[n][:, :], mv[n][:, :, 1], ACT.Sqrt, bias=eps[:, :]).then_inc(ln_sd[n], 1)

            def norm_out(n, b):
                if n == 1:
                    wait(act, mix_set, MULS * b)
                    wait(act, sum_set, TILES * (b - 1))
                else:
                    act.wait_ge(mix_set, MULS * rows_done(b, 1))
                for c in range(G):
                    src = job()
                    nc.scalar.activation(bufB[:, c, 1:T + 1], src[:, :], ACT.Identity, bias=vec(f"ln{n}_b", c),
                                         scale=vec(f"ln{n}_w", c)).then_inc(ln_out[n], 1)

            def low_rank(b):
                wait(act, mul_set, MULS * b)
                wait(act, vhi_set, G * b)
                src = job()
                nc.scalar.activation(t_raw, src[:, :], ACT.Tanh).then_inc(t_set, 1)
                nc.scalar.activation(t_hi.bitcast(F32R), src[:, :], ACT.Tanh).then_inc(t_set, 1)
                if isinstance(b, int) and b == 0:
                    act.wait_ge(mix_w_set, 2)
                else:
                    wait(act, out_stored, 16 * TILES * (b - 1))
                for f in range(4):
                    nc.scalar.activation(t_stack[0:LORA, f, :], src[LORA * f:LORA * f + LORA, :], ACT.Tanh)\
                        .then_inc(t_set, 1)
                act.wait_ge(t_set, TANHS * b + 6)
                nc.scalar.activation(t_stack[LORA:2 * LORA, :, :], t_stack[0:LORA, :, :], ACT.Copy)\
                    .then_inc(t_set, 1)
                src = job()
                for n in range(TILES):
                    nc.scalar.activation(tanhs[tg, P * n:P * n + P], src[LORA * n:LORA * n + LORA, 0:P], ACT.Tanh)\
                        .then_inc(t_set, 1)

            def last_quadrant(b):
                act.wait_ge(lo_set, 4 * (b + 1))
                nc.scalar.activation(t_stack[3 * LORA:, :, :], t_stack[2 * LORA:3 * LORA, :, :], ACT.Copy)\
                    .then_inc(stack_set, 1)

            def decay(b):
                wait(act, e_set, G * b)
                for h in range(2):
                    nc.scalar.activation(tanhs[td, T // 2 * h:T // 2 * (h + 1)],
                                         job()[DECAY * h:DECAY * h + DECAY, 0:T // 2], ACT.Tanh).then_inc(td_set, 1)

            def project(b, g, kind):
                s, par = G * b + g, g % 2
                src = job()
                if kind == "v":
                    wait(act, dv_set, s - 1)
                    nc.scalar.activation(pv[:, par, :], src[:, :], ACT.Copy).then_inc(v_set, 1)
                    wait(act, bc_full, HEAD * (s - 1))
                    if isinstance(s, int) and s == 0:
                        pass
                    elif g > 0:
                        act.wait_ge(stack_in[(g - 1) % 2], stack_loaded(b, g - 1))
                    else:
                        act.wait_ge(stack_in[1], stack_loaded(b - 1, G - 1))
                    nc.scalar.activation(v_hi[:, :], src[:, :], ACT.Copy).then_inc(vhi_set, 1)
                elif kind == "k":
                    wait(act, kv_set, HEAD * (s - 1))
                    wait(act, diag_set, s - 1)
                    nc.scalar.activation(pk[:, par, :], src[:, :], ACT.Copy).then_inc(k_set, 1)
                elif kind == "r":
                    wait(act, rs_set, SLOTS * (s - 1))
                    wait(act, diag_set, s - 1)
                    act.wait_ge(vlo_set, s + 1)
                    nc.scalar.activation(pr[:, par, :], src[:, :], ACT.Copy).then_inc(r_set, 1)
                elif kind == "w":
                    wait(act, scan_set, HEAD * (s - 1))
                    nc.scalar.activation(pw[:, par, :], src[:, :], ACT.Exp, bias=vec("time_decay", g)).then_inc(e_set, 1)
                    act.wait_ge(e_set, s + 1)
                    nc.scalar.activation(pw[:, par, :], pw[:, par, :], ACT.Exp, scale=-1.0).then_inc(w_set, 1)
                else:
                    wait(act, x1_set, TILES * b)
                    nc.scalar.activation(gate[:, g, :], src[:, :], ACT.Tanh, scale=0.5).then_inc(th_set, 1)

            def v_middle(s, g):
                act.wait_ge(vrest_set, s + 1)
                nc.scalar.activation(v_mid[:, :], pr[:, g % 2, :], ACT.Copy).then_inc(vmid_set, 1)

            def centred(s):
                act.wait_ge(cen_full, s + 1)
                nc.scalar.activation(fin_y[:, :], ps_f[:, :], ACT.Copy).then_inc(yc_set, 1)
                wait(act, yn_set, s)
                nc.scalar.activation(fin_s[:, :], ps_f[:, :], ACT.Square).then_inc(sq_set, 1)

            def group_sd(s):
                act.wait_ge(var_full, s + 1)
                nc.scalar.activation(head_sd[:, :, :], ps_f[:, 0:TILES * HG], ACT.Sqrt, bias=eps[:, :]).then_inc(gsd_set, 1)

            def repeat_rs(s):
                act.wait_ge(grs_set, s + 1)
                nc.scalar.activation(fin_s[:, :].rearrange("p (t j h) -> p t j h", t=TILES, j=HEAD),
                                     head_sd[:, :, :].unsqueeze(2).to_broadcast([P, TILES, HEAD, HG]), ACT.Copy)\
                    .then_inc(rep_set, 1)

            def group_affine(s, g):
                act.wait_ge(yn_set, s + 1)
                nc.scalar.activation(fin_y[:, :], fin_y[:, :], ACT.Identity, bias=half_gn[:, 1, g:g + 1]).then_inc(z_set, 1)

            def receptance(b, t):
                nc.scalar.activation(bufB[:, t, 0:T], job()[:, :], ACT.Tanh, scale=0.5).then_inc(rth_set, 1)
                act.wait_ge(rth_set, TILES * b + t + 1)
                nc.scalar.activation(bufB[:, t, 0:T], bufB[:, t, 0:T], ACT.Identity, bias=half[:, :],
                                     scale=0.5).then_inc(rr_set, 1)

            def key(b, f):
                if f == 0:
                    act.wait_ge(rth_set, TILES * (b + 1))
                nc.scalar.activation(bufD[:, f, :], job()[:, :], ACT.Relu).then_inc(relu_set, 1)
                act.wait_ge(relu_set, G * b + f + 1)
                nc.scalar.activation(bufD[:, f, :], bufD[:, f, :], ACT.Square).then_inc(kk_set, 1)

            def row(b, prev, more):
                for slot in range(G * SLOTS):
                    g, i = divmod(slot, SLOTS)
                    s = G * b + g
                    finish = g > 0 or prev
                    if finish and i == FINISH["affine"]:
                        group_affine(s - 1, (g - 1) % G)
                    if finish and i == FINISH["variance"]:
                        group_sd(s - 1)
                    if finish and i == FINISH["rs"]:
                        repeat_rs(s - 1)
                    if prev:
                        if slot == LN2_NORM - 1:
                            norm_sd(2, b - 1)
                        for t in RECEPTANCE_AT.get(slot, ()):
                            receptance(b - 1, t)
                        for f in KEY_AT.get(slot, ()):
                            key(b - 1, f)
                    if more and slot == LN1_NORM - 1:
                        norm_sd(1, b + 1)
                    if more and slot == LOW_RANK:
                        low_rank(b + 1)
                    if more and slot == TANH_REST:
                        last_quadrant(b + 1)
                    if more and slot == DECAY_SLOT:
                        decay(b + 1)
                    for row_, group, kind in projections(b, slot - 1, more):
                        if kind == "v":
                            v_middle(G * row_ + group, group)
                    for at in projections(b, slot, more):
                        project(*at)
                    if finish and i == FINISH["centre"]:
                        centred(s - 1)
                    if prev and slot == LN2_TRANSPOSE:
                        norm_out(2, b - 1)
                    if more and slot == LN1_TRANSPOSE:
                        norm_out(1, b + 1)

            act.wait_ge(consts_set, 2)
            nc.scalar.activation(unread[:, :], eps[:, :], ACT.Sqrt)
            norm_sd(1, 0)
            act.wait_ge(small_in, 16 * len(SMALL))
            act.wait_ge(consts_set, 3)
            norm_out(1, 0)
            low_rank(0)
            last_quadrant(0)
            project(0, 0, "v")
            v_middle(0, 0)
            decay(0)
            for kind in "wkr":
                project(0, 0, kind)
            row(0, False, True)
            with act.Fori(1, BATCH - 1) as b:
                banks.enter(b)
                row(b, True, True)
            banks.leave()
            last = BATCH - 1
            row(last, True, False)
            centred(G * BATCH - 1)
            group_sd(G * BATCH - 1)
            repeat_rs(G * BATCH - 1)
            group_affine(G * BATCH - 1, G - 1)
            norm_sd(2, last)
            norm_out(2, last)
            for t in range(TILES):
                receptance(last, t)
            for f in range(G):
                key(last, f)

        @block.vector
        def _(dve):
            banks = Banks(ps_d, DVE_JOBS)

            def job():
                src, number, _ = banks.take()
                dve.wait_ge(d_full, number)
                return src

            def pair(b, g, i):
                s, par, two = G * b + g, g % 2, state[:, STATE_BUF[i]]
                if i == 0:
                    dve.wait_ge(s0_in, 16 * (s + 1))
                    dve.wait_ge(k_set, s + 1)
                wait(dve, red_done, SLOTS * s + i + 1 - STATE_AGO[i])
                nc.vector.tensor_copy(two[:, :, 0], s0[:, g, 2 * i:2 * i + 2]).then_inc(s0_set, 1)
                for e in range(2):
                    dve.wait_ge(bc_full, HEAD * s + 2 * i + e + 1)
                    nc.vector.tensor_tensor(two[:, e, 1:T + 1], ps_bc[e][:, :], pk[:, par, :], ALU.mult)\
                        .then_inc(kv_set, 1)
                if i == 0:
                    dve.wait_ge(w_set, s + 1)
                dve.wait_ge(s0_set, SLOTS * s + i + 1)
                for e in range(2):
                    dve.wait_ge(kv_set, HEAD * s + 2 * i + e + 1)
                    nc.vector.tensor_tensor_scan(two[:, e, 1:T + 1], pw[:, par, :], two[:, e, 1:T + 1],
                                                 two[:, e, 0:1], ALU.mult, ALU.add).then_inc(scan_set, 1)

            def diagonal(b, g):
                s, par = G * b + g, g % 2
                dve.wait_ge(r_set, s + 1)
                wait(dve, y_set, s)
                wait(dve, yn_set, s)
                nc.vector.scalar_tensor_tensor(diag[:, :], pr[:, par, :], vec("faaaa", g), pk[:, par, :],
                                               ALU.mult, ALU.mult).then_inc(diag_set, 1)

            def diagonal_v(b, g):
                s = G * b + g
                dve.wait_ge(diag_full, s + 1)
                dve.wait_ge(v_set, s + 1)
                nc.vector.tensor_tensor(diag[:, :], ps_f[:, :], pv[:, g % 2, :], ALU.mult).then_inc(dv_set, 1)

            def sum_y(s):
                dve.wait_ge(red_done, SLOTS * (s + 1))
                dve.wait_ge(dv_set, s + 1)
                wait(dve, yg_set, s)
                nc.vector.tensor_tensor(fin_y[:, :], ps_y[:, :], diag[:, :], ALU.add).then_inc(y_set, 1)

            def group_rs(s):
                dve.wait_ge(gsd_set, s + 1)
                nc.vector.reciprocal(head_sd[:, :, :], head_sd[:, :, :]).then_inc(grs_set, 1)

            def normalise_y(s, g):
                dve.wait_ge(rs_full, s + 1)
                dve.wait_ge(sq_set, s + 1)
                nc.vector.scalar_tensor_tensor(fin_y[:, :], fin_y[:, :], half_gn[:, 0, g:g + 1], ps_f[:, :],
                                               ALU.mult, ALU.mult).then_inc(yn_set, 1)

            def gate_silu(b, g):
                dve.wait_ge(th_set, G * b + g + 1)
                nc.vector.scalar_tensor_tensor(gate[:, g, :], gate[:, g, :], 1.0,
                                               gate_bank[g][:, :], ALU.add, ALU.mult).then_inc(gate_set, 1)

            def norm_stats(n, src, b, t):
                nc.vector.bn_stats(stats[n][:, t, :], src[:, t, :]).then_inc(ln_stats[n], 1)

            def norm_aggr(n, b):
                dve.wait_ge(ln_stats[n], TILES * (b + 1))
                nc.vector.memset(wait_carrier[:, :], 0.0)
                for t in range(TILES):
                    nc.vector.bn_aggr(mv[n][:, t, :], stats[n][:, t, :]).then_inc(ln_aggr[n], 1)

            def norm(n, src, b):
                dve.wait_ge(ln_sd[n], b + 1)
                nc.vector.reciprocal(sd[n][:, :], sd[n][:, :]).then_inc(ln_rs[n], 1)
                dve.wait_ge(ln_rs[n], b + 1)
                if n == 2:
                    dve.wait_ge(td_set, 2 * rows_done(b, 1))
                for t in range(TILES):
                    nc.vector.tensor_scalar({1: x_next, 2: bufA}[n][:, t, :], src[:, t, :], mv[n][:, t, 0:1], sd[n][:, t:t + 1],
                                            ALU.subtract, ALU.mult).then_inc(ln_norm[n], 1)

            def shift(n, b, done):
                dve.wait_ge(ln_edge[n], b + 1)
                if n == 1:
                    wait(dve, rk_set, TILES * (b - 1))
                    wait(dve, mul_set, MULS * b)
                else:
                    dve.wait_ge(mul_set, MULS * rows_done(b, 1))
                for c in range(G):
                    dve.wait_ge(ln_out[n], G * b + c + 1)
                    nc.vector.tensor_tensor(bufD[:, c, :], bufB[:, c, 0:T], bufB[:, c, 1:T + 1], ALU.subtract)\
                        .then_inc(done, 1)

            def low_rank_in(b):
                if isinstance(b, int) and b < 2:
                    wait(dve, td_set, 2 * b)
                else:
                    wait(dve, relu_set, G * (b - 1))
                for c in range(G):
                    dve.wait_ge(sx_set, G * b + c + 1)
                    nc.vector.scalar_tensor_tensor(xxx[:, c, :], bufD[:, c, :], vec("maa_x", c), bufB[:, c, 1:T + 1],
                                                   ALU.mult, ALU.add).then_inc(xxx_set, 1)

            def tanh_rest(b):
                dve.wait_ge(t_set, TANHS * b + 2)
                if isinstance(b, int) and b == 0:
                    dve.wait_ge(mix_w_set, 2)
                else:
                    wait(dve, out_stored, 16 * TILES * (b - 1))
                for f in range(4):
                    rows = slice(LORA * f, LORA * f + LORA)
                    nc.vector.tensor_tensor(t_stack[2 * LORA:3 * LORA, f, :], t_raw[rows, :], t_hi[rows, :],
                                            ALU.subtract).then_inc(lo_set, 1)

            def mixes(b, kind, chunks=range(G)):
                if kind == "w":
                    dve.wait_ge(t_set, TANHS * (b + 1))
                else:
                    wait(dve, {"v": vhi_set, "k": k_set, "r": r_set, "g": gate_set}[kind], G * b)
                for c in chunks:
                    src = job()
                    nc.vector.scalar_tensor_tensor(mixed[kind][:, c, :], src[:, :], vec(f"maa_{kind}", c), bufD[:, c, :],
                                                   ALU.add, ALU.mult).then_inc(mul_set, 1)

            def residual(b, t):
                if t == 0:
                    dve.wait_ge(res_in, 16 * (b + 1))
                src = job()
                nc.vector.tensor_tensor(x1[:, t, :], src[:, :], x1[:, t, :], ALU.add).then_inc(x1_set, 1)
                dve.wait_ge(x1_set, TILES * b + t + 1)
                norm_stats(2, x1, b, t)

            def channel_mix(b, name, into, done):
                for c in range(G):
                    if name == "fmaa_k":
                        dve.wait_ge(sxc_set, G * b + c + 1)
                    nc.vector.scalar_tensor_tensor(into[:, c, :], bufD[:, c, :], vec(name, c), bufB[:, c, 1:T + 1],
                                                   ALU.mult, ALU.add).then_inc(done, 1)

            def key_mix(b):
                dve.wait_ge(ln_out[2], G * (b + 1))
                channel_mix(b, "fmaa_k", bufA, xk_set)

            def receptance_mix(b):
                dve.wait_ge(xk_set, G * (b + 1))
                channel_mix(b, "fmaa_r", bufD, xr_set)

            def value(b, t):
                dve.wait_ge(rr_set, TILES * b + t + 1)
                src = job()
                nc.vector.tensor_tensor(bufB[:, t, 0:T], src[:, :], bufB[:, t, 0:T], ALU.mult).then_inc(rk_set, 1)

            def row(b, prev, more):
                for slot in range(G * SLOTS):
                    g, i = divmod(slot, SLOTS)
                    s = G * b + g
                    finish = g > 0 or prev
                    if finish and i == 1:
                        sum_y(s - 1)
                    pair(b, g, i)
                    if finish and i == FINISH["rs"]:
                        group_rs(s - 1)
                    if finish and i == FINISH["normalise"]:
                        normalise_y(s - 1, (g - 1) % G)
                    if i == FINISH["diagonal"]:
                        diagonal(b, g)
                    if i == FINISH["diagonal_v"]:
                        diagonal_v(b, g)
                    for row_, group, kind in projections(b, slot, more):
                        if kind == "g":
                            gate_silu(row_, group)
                    if more and slot == TANH_REST:
                        tanh_rest(b + 1)
                    for at in halves(b, slot, more)[:1]:
                        mixes(*at)
                    if prev:
                        for t in OUT_AT.get(slot, ()):
                            residual(b - 1, t)
                        if slot == LN2_NORM - 1:
                            norm_aggr(2, b - 1)
                        if slot == LN2_NORM:
                            norm(2, x1, b - 1)
                        if slot == KEY_MIX:
                            shift(2, b - 1, sxc_set)
                            key_mix(b - 1)
                        if slot == RECEPTANCE_MIX:
                            receptance_mix(b - 1)
                        for t in VALUE_AT.get(slot, ()):
                            value(b - 1, t)
                    for at in halves(b, slot, more)[1:]:
                        mixes(*at)
                    if more and slot == LN1_STATS:
                        for t in range(TILES):
                            dve.wait_ge(x_in[t], 16 * (b + 2))
                            norm_stats(1, x_next, b + 1, t)
                        norm_aggr(1, b + 1)
                    if more and slot == LN1_NORM:
                        norm(1, x_next, b + 1)
                    if more and slot == LOW_RANK_IN:
                        shift(1, b + 1, sx_set)
                        low_rank_in(b + 1)

            nc.vector.memset(eps[:, :], EPS).then_inc(consts_set, 1)
            nc.vector.memset(half[:, :], 0.5).then_inc(consts_set, 1)
            for t in range(TILES):
                dve.wait_ge(x_in[t], 16)
                norm_stats(1, x_next, 0, t)
            norm_aggr(1, 0)
            dve.wait_ge(small_in, 16 * len(SMALL))
            n = VECS.index("gn_w")
            nc.vector.tensor_scalar(half_gn[:, :, :], vecs[:, n:n + 2, :], 0.5, None, ALU.mult).then_inc(consts_set, 1)
            norm(1, x_next, 0)
            shift(1, 0, sx_set)
            low_rank_in(0)
            dve.wait_ge(w_hi_set, 1)
            for q in (1, 3):
                rows = slice(LORA * q, LORA * q + LORA)
                nc.vector.tensor_tensor(mix_w[rows, :, :], x1[rows, :, :], mix_w[rows, :, :].bitcast(F32),
                                        ALU.subtract).then_inc(mix_w_set, 1)
            tanh_rest(0)
            for kind in MIX_ORDER[:-1]:
                mixes(0, kind)
                if kind in "kr":
                    dve.wait_ge(mix_set, G * MIX_ORDER.index(kind))
                    for c in range(G):
                        dve.wait_ge(mul_set, G * MIX_ORDER.index(kind) + c + 1)
                        nc.vector.tensor_tensor(mixed[kind][:, c, :], mixed[kind][:, c, :], bufB[:, c, 1:T + 1], ALU.add)\
                            .then_inc(mix_set, 1)
            row(0, False, True)
            with dve.Fori(1, BATCH - 1) as b:
                banks.enter(b)
                row(b, True, True)
            banks.leave()
            last = BATCH - 1
            row(last, True, False)
            sum_y(G * BATCH - 1)
            group_rs(G * BATCH - 1)
            normalise_y(G * BATCH - 1, G - 1)
            for t in range(TILES):
                residual(last, t)
            norm_aggr(2, last)
            norm(2, x1, last)
            shift(2, last, sxc_set)
            key_mix(last)
            receptance_mix(last)
            for t in range(TILES):
                value(last, t)

        @block.gpsimd
        def _(pool):
            def read_out(b, g, i):
                s = G * b + g
                if i == 0:
                    pool.wait_ge(r_set, s + 1)
                pool.wait_ge(scan_set, HEAD * s + 2 * i + 2)
                nc.gpsimd.tensor_tensor(state[:, STATE_BUF[i], :, 0:T], state[:, STATE_BUF[i], :, 0:T],
                                        pr[:, g % 2, :].unsqueeze(1).to_broadcast([P, 2, T]), ALU.mult)\
                    .then_inc(rs_set, 1)

            def v_less_first(s, g):
                wait(pool, rs_set, SLOTS * (s - 1))
                wait(pool, diag_set, s - 1)
                pool.wait_ge(vhi_set, s + 1)
                nc.gpsimd.tensor_tensor(pr[:, g % 2, :], pv[:, g % 2, :], v_hi[:, :], ALU.subtract).then_inc(vrest_set, 1)

            def v_third(s, g):
                pool.wait_ge(vmid_set, s + 1)
                nc.gpsimd.tensor_tensor(v_lo[:, :], pr[:, g % 2, :], v_mid[:, :], ALU.subtract).then_inc(vlo_set, 1)

            def gated_y(b, g):
                s = G * b + g
                pool.wait_ge(z_set, s + 1)
                pool.wait_ge(gate_set, s + 1)
                nc.gpsimd.tensor_tensor(gate[:, g, :], fin_y[:, :], gate[:, g, :], ALU.mult).then_inc(yg_set, 1)

            def edge(n, b):
                if n == 1:
                    wait(pool, mix_set, MULS * b)
                    wait(pool, sum_set, TILES * (b - 1))
                else:
                    pool.wait_ge(mix_set, MULS * rows_done(b, 1))
                nc.gpsimd.tensor_copy(bufB[:, :, 0], small["states"][:, b, n - 1, :]).then_inc(ln_edge[n], 1)

            def mixes(b, kind, chunks=range(G)):
                for c in chunks:
                    pool.wait_ge(mul_set, MULS * b + G * MIX_ORDER.index(kind) + c + 1)
                    nc.gpsimd.tensor_tensor(mixed[kind][:, c, :], mixed[kind][:, c, :], bufB[:, c, 1:T + 1], ALU.add)\
                        .then_inc(mix_set, 1)

            def total(b, t):
                pool.wait_ge(rk_set, TILES * b + t + 1)
                nc.gpsimd.tensor_tensor(x1[:, t, :], x1[:, t, :], bufB[:, t, 0:T], ALU.add).then_inc(sum_set, 1)

            def row(b, prev, more):
                for slot in range(G * SLOTS):
                    g, i = divmod(slot, SLOTS)
                    s = G * b + g
                    finish = g > 0 or prev
                    read_out(b, g, i)
                    if finish and i == FINISH["gated"]:
                        gated_y(*((b, g - 1) if g > 0 else (b - 1, G - 1)))
                    for row_, group, kind in projections(b, slot - 1, more):
                        if kind == "v":
                            v_third(G * row_ + group, group)
                    for row_, group, kind in projections(b, slot, more):
                        if kind == "v":
                            v_less_first(G * row_ + group, group)
                    for at in halves(b, slot, more):
                        mixes(*at)
                    if prev and slot == LN2_TRANSPOSE:
                        edge(2, b - 1)
                    if prev:
                        for t in TOTAL_AT.get(slot, ()):
                            total(b - 1, t)
                    if more and slot == LN1_TRANSPOSE:
                        edge(1, b + 1)

            pool.wait_ge(small_in, 16 * len(SMALL))
            edge(1, 0)
            pool.wait_ge(mix_w_in, 16)
            nc.gpsimd.tensor_copy(mix_w[:, :, :], x1[:, :, :]).then_inc(w_hi_set, 1)
            mixes(0, "v")
            mixes(0, "w")
            v_less_first(0, 0)
            v_third(0, 0)
            row(0, False, True)
            with pool.Fori(1, BATCH - 1) as b:
                row(b, True, True)
            last = BATCH - 1
            row(last, True, False)
            gated_y(last, G - 1)
            edge(2, last)
            for t in range(TILES):
                total(last, t)


def kernel(**inputs):
    import ml_dtypes
    import concourse.bacc as bacc
    from concourse.bass_utils import run_bass_kernel_spmd

    a = {k.replace("L0_xattn_", ""): np.asarray(v) for k, v in inputs.items()}
    jh = np.arange(C).reshape(G, HG, HEAD).transpose(0, 2, 1).reshape(C)

    def chunks(w):
        return np.ascontiguousarray(w.reshape(-1, P, w.shape[1]).transpose(1, 0, 2))

    def channel_major(v):
        v = v.reshape(v.shape[:-1] + (G, P))
        return np.moveaxis(v, -1, 0)

    vectors = dict(a, faaaa=a["faaaa"].reshape(C), gn_w=a["gn_w"][jh], gn_b=a["gn_b"][jh])
    ctx_rows = a["ctx_2048"]
    eye, row, col = np.eye(P, dtype=np.float32), np.arange(P)[:, None], np.arange(P)[None, :]
    same_head = (row % HG == col % HG).astype(np.float32)
    arrays = {
        "x": a["x"],
        "vecs": np.stack([channel_major(vectors[n]) for n in VECS], axis=1),
        "lora1": chunks(a["maa_w1"]),
        "lora2": np.tile(a["maa_w2"][:4].transpose(1, 0, 2), (4, 1, 1)),
        "dec1": chunks(a["decay_w1"]),
        "second": np.concatenate([a["decay_w2"], a["maa_w2"][4]]),
        "ident": eye,
        "sel_v": np.stack([((np.arange(96)[:, None] % 32) == HG * jj + col // HEAD) for jj in range(J4)], axis=1)
        .astype(ml_dtypes.bfloat16),
        "sel_r": np.stack([(np.arange(32)[None, :] == HG * jj + row // HEAD) for jj in range(J4)], axis=1)
        .astype(np.float32),
        "ones": (row // HEAD == col % HG).astype(np.float32),
        "avg": (row % HG == col[:, :HG]).astype(np.float32) / HEAD,
        "center": eye - same_head / HEAD,
        "states": channel_major(ctx_rows[:, [1, 0]]),
        "s0": ctx_rows[:, 2:2 + HEAD].reshape(BATCH, G, P, HEAD).transpose(2, 0, 1, 3),
        "Wv": chunks(a["Wv"].T[:, jh]), "Wg": chunks(a["Wg"].T[:, jh]),
        "Wk": chunks(a["Wk"].T), "Wr": chunks(a["Wr"].T), "Wo": chunks(a["Wo"].T[jh]),
        "fWr": chunks(a["fWr"].T), "fWk": chunks(a["fWk"].T), "fWv": chunks(a["fWv"].T),
    }
    arrays = {k: np.ascontiguousarray(v) for k, v in arrays.items()}
    nc = bacc.Bacc("TRN2", target_bir_lowering=False, num_devices=1)
    dram = {n: nc.dram_tensor(f"in_{n}", v.shape, mybir.dt.from_np(v.dtype), kind="ExternalInput").ap()
            for n, v in arrays.items()}
    out = nc.dram_tensor("out_0", (BATCH, T, C), F32, kind="ExternalOutput").ap()
    build(nc, dram, out)
    r = run_bass_kernel_spmd(nc, [{f"in_{n}": v for n, v in arrays.items()}], core_ids=[0])
    return r.results[0]["out_0"]
```
